# Optimizing a Trainium2 kernel written in Bass

```python
import numpy as np
import jax
import jax.numpy as jnp

def _softmax(x, axis=-1):
    return jax.nn.softmax(x, axis=axis)
def _gelu(x):
    return jax.nn.gelu(x, approximate=True)
def _silu(x):
    return jax.nn.silu(x)
def _sigmoid(x):
    return jax.nn.sigmoid(x)
def _layernorm(x, axis=-1, eps=1e-5):
    m = jnp.mean(x, axis=axis, keepdims=True)
    v = jnp.var(x, axis=axis, keepdims=True)
    return (x - m) / jnp.sqrt(v + eps)
def _scatter_add(tgt, idx, src, axis=0):
    return tgt.at[idx].add(src)
def _segment_sum(src, seg, n):
    return jax.ops.segment_sum(src, seg, n)

kernel_name = 'mk_adj_preln_d4_adj_512_b6158b'

def setup_inputs(seed: int = 0):
    np.random.seed(seed)
    _w = jnp.asarray
    def _rec_inputs():
        import jax
        import jax.numpy as jnp
        _gk = jax.random.key(seed)
        x = -0.0002928 + 1 * jax.random.normal(jax.random.fold_in(_gk, 1), (2708, 512), jnp.float32)
        _a = jax.random.bernoulli(jax.random.fold_in(_gk, 2), 0.0014771, (2708, 2708))
        _a = jnp.logical_or(_a, jnp.swapaxes(_a, -1, -2))
        _a = jnp.logical_or(_a, jnp.eye(2708, dtype=bool))
        adj = _a.astype(jnp.int32)
        return x, adj
    x, adj = _rec_inputs()
    def _L0_gnn_setup():
        import jax, jax.numpy as jnp
        import numpy as np
        N = 8192
        D_IN = 512
        D_OUT = 512
        key = jax.random.key(seed)
        k1, k2, k3, k4 = jax.random.split(key, 4)
        node_feats = jax.random.normal(k1, (N, D_IN), dtype=jnp.float32)
        adj_matrix = jax.random.randint(k2, (N, N), 0, 2, dtype=jnp.int32)
        w_self = jax.random.normal(k3, (D_OUT, D_IN), dtype=jnp.float32) * D_IN ** (-0.5)
        w_neigh = jax.random.normal(k4, (D_OUT, D_IN), dtype=jnp.float32) * D_IN ** (-0.5)
        return {'node_feats': node_feats, 'adj_matrix': adj_matrix, 'w_self': w_self, 'w_neigh': w_neigh}
    _L0_gnn_all = _L0_gnn_setup()
    _L0_gnn_in = {k: v for k, v in _L0_gnn_all.items() if k in ('w_self', 'w_neigh', )}
    del _L0_gnn_all

    def _L1_gnn_setup():
        import jax, jax.numpy as jnp
        import numpy as np
        N, D_IN, D_OUT = (8192, 512, 512)
        key = jax.random.key(seed)
        ks = jax.random.split(key, 8)
        scale_in = 1.0 / np.sqrt(D_IN)
        scale_cat = 1.0 / np.sqrt(2 * D_OUT)
        return {'x': jax.random.normal(ks[0], (N, D_IN), dtype=jnp.float32), 'adj': jax.random.randint(ks[1], (N, N), 0, 2, dtype=jnp.int32), 'W_self': jax.random.uniform(ks[2], (D_IN, D_OUT), jnp.float32, -scale_in, scale_in), 'b_self': jax.random.uniform(ks[3], (D_OUT,), jnp.float32, -scale_in, scale_in), 'W_nb': jax.random.uniform(ks[4], (D_IN, D_OUT), jnp.float32, -scale_in, scale_in), 'b_nb': jax.random.uniform(ks[5], (D_OUT,), jnp.float32, -scale_in, scale_in), 'W_comb': jax.random.uniform(ks[6], (2 * D_OUT, D_OUT), jnp.float32, -scale_cat, scale_cat), 'b_comb': jax.random.uniform(ks[7], (D_OUT,), jnp.float32, -scale_cat, scale_cat)}
    _L1_gnn_all = _L1_gnn_setup()
    _L1_gnn_in = {k: v for k, v in _L1_gnn_all.items() if k in ('W_self', 'b_self', 'W_nb', 'b_nb', 'W_comb', 'b_comb', )}
    del _L1_gnn_all

    def _L2_gnn_setup():
        import jax, jax.numpy as jnp
        import numpy as np
        key = jax.random.key(seed)
        kX, kA, k1, k2, k3, k4 = jax.random.split(key, 6)
        N, Cin, Cout = (8192, 512, 512)
        X = jax.random.normal(kX, (N, Cin), dtype=jnp.float32)
        A = jax.random.randint(kA, (N, N), 0, 2, dtype=jnp.int32)
        bound = 1.0 / np.sqrt(Cin)
        W_nb = jax.random.uniform(k1, (Cout, Cin), jnp.float32, -bound, bound)
        b_nb = jax.random.uniform(k2, (Cout,), jnp.float32, -bound, bound)
        W_line = jax.random.uniform(k3, (Cout, Cin), jnp.float32, -bound, bound)
        b_line = jax.random.uniform(k4, (Cout,), jnp.float32, -bound, bound)
        return {'X': X, 'A': A, 'W_nb': W_nb, 'b_nb': b_nb, 'W_line': W_line, 'b_line': b_line, 'neibor_num': 64}
    _L2_gnn_all = _L2_gnn_setup()
    _L2_gnn_in = {k: v for k, v in _L2_gnn_all.items() if k in ('W_nb', 'b_nb', 'W_line', 'b_line', )}
    del _L2_gnn_all

    def _L3_gnn_setup():
        import jax, jax.numpy as jnp
        import numpy as np
        N, IN_DIM, HEADS, OUT_DIM = (3072, 512, 8, 64)
        ALPHA = 0.2
        NEG_INF = jnp.float32(-9000000000000000.0)
        key = jax.random.key(seed)
        k1, k2, k3, k4, k5 = jax.random.split(key, 5)
        x = jax.random.normal(k1, (N, IN_DIM), dtype=jnp.float32)
        adj = jax.random.randint(k2, (N, N), 0, 2, dtype=jnp.int32)
        bw = 1.414 * float(np.sqrt(6.0 / (IN_DIM + OUT_DIM)))
        W = jax.random.uniform(k3, (HEADS, IN_DIM, OUT_DIM), dtype=jnp.float32, minval=-bw, maxval=bw)
        ba = 1.414 * float(np.sqrt(6.0 / (2 * OUT_DIM + 1)))
        a1 = jax.random.uniform(k4, (HEADS, OUT_DIM), dtype=jnp.float32, minval=-ba, maxval=ba)
        a2 = jax.random.uniform(k5, (HEADS, OUT_DIM), dtype=jnp.float32, minval=-ba, maxval=ba)
        return {'x': x, 'adj': adj, 'W': W, 'a1': a1, 'a2': a2}
    _L3_gnn_all = _L3_gnn_setup()
    _L3_gnn_in = {k: v for k, v in _L3_gnn_all.items() if k in ('W', 'a1', 'a2', )}
    del _L3_gnn_all

    return {
        "x": x,
        "adj": adj,
        "L0_gnn_w_self": _L0_gnn_in["w_self"],
        "L0_gnn_w_neigh": _L0_gnn_in["w_neigh"],
        "L1_gnn_W_self": _L1_gnn_in["W_self"],
        "L1_gnn_b_self": _L1_gnn_in["b_self"],
        "L1_gnn_W_nb": _L1_gnn_in["W_nb"],
        "L1_gnn_b_nb": _L1_gnn_in["b_nb"],
        "L1_gnn_W_comb": _L1_gnn_in["W_comb"],
        "L1_gnn_b_comb": _L1_gnn_in["b_comb"],
        "L2_gnn_W_nb": _L2_gnn_in["W_nb"],
        "L2_gnn_b_nb": _L2_gnn_in["b_nb"],
        "L2_gnn_W_line": _L2_gnn_in["W_line"],
        "L2_gnn_b_line": _L2_gnn_in["b_line"],
        "L3_gnn_W": _L3_gnn_in["W"],
        "L3_gnn_a1": _L3_gnn_in["a1"],
        "L3_gnn_a2": _L3_gnn_in["a2"],
    }

def reference(x, adj, L0_gnn_w_self, L0_gnn_w_neigh, L1_gnn_W_self, L1_gnn_b_self, L1_gnn_W_nb, L1_gnn_b_nb, L1_gnn_W_comb, L1_gnn_b_comb, L2_gnn_W_nb, L2_gnn_b_nb, L2_gnn_W_line, L2_gnn_b_line, L3_gnn_W, L3_gnn_a1, L3_gnn_a2):
    import jax
    import jax.numpy as jnp
    def _L0_gnn_ref(node_feats, adj_matrix, w_self, w_neigh):
        import jax, jax.numpy as jnp
        import numpy as np
        N = 8192
        D_IN = 512
        D_OUT = 512
        adj_f = adj_matrix.astype(node_feats.dtype)
        s = adj_f @ node_feats[:, 0]
        has_neigh = jnp.sum(adj_matrix, axis=1) > 0
        s = jnp.where(has_neigh, s, jnp.zeros_like(s))
        neigh_term = s[:, None] * jnp.sum(w_neigh, axis=1)[None, :]
        return jax.nn.relu(node_feats @ w_self.T + neigh_term)

    def _L1_gnn_ref(x, adj, W_self, b_self, W_nb, b_nb, W_comb, b_comb):
        import jax, jax.numpy as jnp
        import numpy as np
        N, D_IN, D_OUT = (8192, 512, 512)
        mask = (adj > 0).astype(x.dtype)
        deg = jnp.sum(mask, axis=1, keepdims=True)
        agg = mask @ x / jnp.maximum(deg, 1.0)
        self_f = x @ W_self + b_self
        nb_f = agg @ W_nb + b_nb
        combined = jnp.concatenate([self_f, nb_f], axis=-1)
        out = combined @ W_comb + b_comb
        return jax.nn.relu(out)

    def _L2_gnn_ref(X, A, W_nb, b_nb, W_line, b_line, neibor_num):
        import jax, jax.numpy as jnp
        import numpy as np
        Ab = A > 0
        keep = Ab & (jnp.cumsum(Ab.astype(jnp.int32), axis=1) <= neibor_num)
        cnt = keep.sum(axis=1, keepdims=True).astype(X.dtype)
        nb_sum = keep.astype(X.dtype) @ X
        nb_mean = nb_sum / jnp.maximum(cnt, 1.0)
        xj = jax.nn.leaky_relu(nb_mean @ W_nb.T + b_nb)
        xi = jax.nn.leaky_relu(X @ W_line.T + b_line)
        return xi + jnp.where(cnt > 0, xj, jnp.zeros((), X.dtype))

    def _L3_gnn_ref(x, adj, W, a1, a2):
        import jax, jax.numpy as jnp
        import numpy as np
        N, IN_DIM, HEADS, OUT_DIM = (3072, 512, 8, 64)
        ALPHA = 0.2
        NEG_INF = jnp.float32(-9000000000000000.0)
        Wh = jnp.einsum('nd,hdo->hno', x, W)
        f1 = jnp.einsum('hno,ho->hn', Wh, a1)
        f2 = jnp.einsum('hno,ho->hn', Wh, a2)
        e = jax.nn.leaky_relu(f1[:, :, None] + f2[:, None, :], negative_slope=ALPHA)
        e = jnp.where(adj[None, :, :] > 0, e, NEG_INF)
        attention = jax.nn.softmax(e, axis=-1)
        h_prime = jnp.einsum('hnm,hmo->hno', attention, Wh)
        out = jax.nn.elu(h_prime)
        return jnp.transpose(out, (1, 0, 2)).reshape(x.shape[0], HEADS * OUT_DIM)

    h = jnp.maximum(_layernorm(x, axis=-1), 0.0)
    x = x + _L0_gnn_ref(h, adj, L0_gnn_w_self, L0_gnn_w_neigh)
    h = jnp.maximum(_layernorm(x, axis=-1), 0.0)
    x = x + _L1_gnn_ref(h, adj, L1_gnn_W_self, L1_gnn_b_self, L1_gnn_W_nb, L1_gnn_b_nb, L1_gnn_W_comb, L1_gnn_b_comb)
    h = jnp.maximum(_layernorm(x, axis=-1), 0.0)
    x = x + _L2_gnn_ref(h, adj, L2_gnn_W_nb, L2_gnn_b_nb, L2_gnn_W_line, L2_gnn_b_line, 64)
    h = jnp.maximum(_layernorm(x, axis=-1), 0.0)
    x = x + _L3_gnn_ref(h, adj, L3_gnn_W, L3_gnn_a1, L3_gnn_a2)
    return x


_drawn_inputs = setup_inputs


def setup_inputs(seed=0):
    import zlib

    import numpy as np

    out = dict(_drawn_inputs(seed))
    spreads = {}
    factors = {'L1_gnn_b_self': 32.75,
     'L1_gnn_b_nb': 29.513,
     'L1_gnn_b_comb': 8.0,
     'L2_gnn_b_nb': 8.0,
     'L2_gnn_b_line': 8.0}
    for name, (base, spread) in spreads.items():
        noise = np.random.default_rng([zlib.crc32(name.encode()), seed]).standard_normal(out[name].shape)
        drawn = base * np.exp(spread * noise) if base else spread * noise
        out[name] = jnp.asarray(drawn.astype(out[name].dtype))
    for name, factor in factors.items():
        out[name] = (out[name] * factor).astype(out[name].dtype)
    return out
```

```python
import concourse.bass as bass
from concourse import mybir
from contextlib import ExitStack

DT = mybir.dt
ALU = mybir.AluOpType
ACT = mybir.ActivationFunctionType
AX = mybir.AxisListType
RMAX = bass.bass_isa.ReduceOp.max

P = 128
N = 2708
D = 512
NT = (N + P - 1) // P
NP = NT * P
TAIL = N - (NT - 1) * P
KT = D // P
H, O = 8, 64
OC = O + 1
MC = 96
PB = D // MC
NB = (NT + PB - 1) // PB
KEEP = 64
EPS = 1e-5

H_SCALE = 2.0 ** 11
W_SCALE = 2.0 ** 8
Y_SCALE = 2.0 ** 8
UNSCALE = 1.0 / (H_SCALE * W_SCALE)
EDGE = 2.0


def pipeline(eng, stages, period=2):
    high, low = max(l for l, _ in stages), min(l for l, _ in stages)
    first, last = period - low, NT - 2 - high
    turns = max(0, (last - first + 1) // period)

    def step(u, base):
        for lead, fn in stages:
            if isinstance(u, int):
                if 0 <= u + lead < NT:
                    fn(u + lead, (u + lead) % period)
            else:
                fn(u + lead, (base + lead) % period)

    for u in range(-high, first):
        step(u, u)
    if turns > 0:
        with eng.Fori(first, first + (turns - 1) * period + 1, period) as u:
            for k in range(period):
                step(u + k, first + k)
    for u in range(first + turns * period, NT - low):
        step(u, u)


def inner(t, least):
    return not isinstance(t, int) or t >= least


def gnn_program(nc, x_in, adj, w_self0, w_neigh0, w_self1, b_self1, w_nb1, b_nb1, w_comb, b_comb,
                w_nb2, b_nb2, w_line2, b_line2, w3, a1, a2, out):
    ctx = ExitStack()
    with ctx:
        f32, f16, bf16, u8, i32 = DT.float32, DT.float16, DT.bfloat16, DT.uint8, DT.int32

        def sb(name, shape, dt):
            return ctx.enter_context(nc.sbuf_tensor(name, shape, dt))

        sems = {}

        def S(name):
            if name not in sems:
                sems[name] = ctx.enter_context(nc.semaphore(name))
            return sems[name]

        w_parts = nc.dram_tensor("w_parts", [6, P, 2 * KT * D], f16).ap()
        self_rows = nc.dram_tensor("self_rows", [NT, P, D], f32).ap()
        h0_row = nc.dram_tensor("h0_row", [NT, P], f32).ap()
        ratio_rows = nc.dram_tensor("ratio_rows", [H * NT, P], f32).ap()
        ratio_flat = ratio_rows.rearrange("a b -> (a b)")

        V = sb("neigh_code", [P, NT, NP], u8)
        X = sb("residual", [P, NT, D], f32)
        Yr = sb("products", [P, NT * H * OC + MC - OC], f32)
        Z = sb("arena", [P, 14080], f32)
        SMALL = sb("small", [P, 416], f32)

        def carve(region, byte, shape, dt):
            size = {f32: 4, i32: 4, f16: 2, bf16: 2, u8: 1}[dt]
            count = 1
            for n in shape:
                count *= n
            v = region[:, byte // 4: byte // 4 + (count * size + 3) // 4].bitcast(dt)
            if len(shape) == 1:
                return v
            names = "abcd"[:len(shape)]
            return v.rearrange(f"p ({' '.join(names)}) -> p {' '.join(names)}", **dict(zip(names[1:], shape[1:])))

        Vf = V[:, :, :].rearrange("p a b -> p (a b)").bitcast(f32)
        Xf = X[:, :, :].rearrange("p a b -> p (a b)")
        own0 = Yr[:, 0:NT * D].rearrange("p (t n) -> p t n", n=D)
        Y = Yr[:, 0:NT * D].bitcast(f16).rearrange("p (t s n) -> p t s n", s=2, n=D)
        Wh = Yr[:, 0:NT * H * OC].rearrange("p (h t o) -> p h t o", h=H, o=OC)

        Wt = carve(Z, 0, [2, 2, KT, D], f16)
        xn = carve(Z, 16384, [2, D], f32)
        h_hi = carve(Z, 20480, [2, D], f16)
        h_lo = carve(Z, 22528, [2, D], f16)
        hT = carve(Z, 24576, [2, 2 * KT, P], f16)
        stage = carve(Z, 28672, [2, D], f32)
        blk = carve(Z, 32768, [2, NT, P], bf16)
        tmpa = carve(Z, 44032, [D], f32)
        tmpb = carve(Z, 46080, [D], f32)
        biasC = carve(Z, 48384, [D], f32)
        biasA = carve(Z, 51200, [D], f32)
        biasB = carve(Z, 53248, [D], f32)
        ident_f = carve(Z, 55296, [P], f32)
        ident_h = carve(Z, 55808, [P], f16)
        ident_b = carve(Z, 56064, [P], bf16)
        mask = carve(Z, 0, [2, NP], bf16)
        maskT = carve(Z, 11264, [2, NT, P], bf16)
        pick = carve(Z, 22528, [NT, P], bf16)
        h0_all = carve(Z, 28160, [NP], f32)
        junk_s = carve(Z, 39424, [2816], bf16)
        junk_v = carve(Z, 45056, [2816], bf16)
        adj_in = carve(Xf, 0, [4, N], i32)
        prob = [carve(Z, 11264 * k, [NP], f32) for k in range(3)]
        ratio = [carve(Z, 33792 + 11264 * k, [NP], f32) for k in range(2)]
        f1 = carve(Z, 32768, [H, NT], f32)
        f2 = carve(Z, 33472, [H, NT], f32)
        fmax = carve(Z, 34176, [2, H], f32)
        gmax = carve(Z, 34240, [2, H], f32)
        zmax = carve(Z, 34304, [H], f32)
        guard = carve(Z, 34336, [H], f32)
        rbias = carve(Z, 34368, [H], f32)
        rarg = carve(Z, 34400, [H, NT], f32)
        barg = carve(Z, 35104, [H, NT], f32)
        darg = carve(Z, 35808, [H, NT], f32)
        rexp = carve(Z, 36512, [H, NT], f32)
        dexp = carve(Z, 37216, [H, NT], f32)
        rT = carve(Z, 37920, [2, P], f32)
        ones_f = carve(Z, 38944, [P], f32)
        mean_lo = carve(Z, 39456, [D], f32)
        mean_hi = carve(Z, 41504, [D], f32)
        raw = carve(Yr, 0, [5, KT, D], f32)
        a12 = carve(Yr, 40960, [2, D], f32)
        wc = carve(Vf, 0, [2, KT, D], f32)
        wT = carve(Vf, 16384, [2, KT, D], f32)
        wP = carve(Vf, 32768, [KT, D], f32)
        parts = [carve(Vf, 40960 + 8192 * k, [2, KT, D], f16) for k in range(2)]
        bcols = carve(Vf, 57344, [KT, P], f32)
        rcols = carve(Vf, 59392, [KT, P], f32)
        bcol = carve(Vf, 61440, [2, KT], f32)
        rsum4 = carve(Vf, 61472, [KT], f32)
        fw32 = carve(Vf, 61488, [KT, 2 * H], f32)
        s_col = carve(SMALL, 0, [NT], f32)
        rowsum = carve(SMALL, 88, [NT], f32)
        deg = carve(SMALL, 176, [NT], f32)
        rdeg = carve(SMALL, 264, [NT], f32)
        rcnt = carve(SMALL, 352, [NT], f32)
        has = carve(SMALL, 440, [NT], f32)
        iso = carve(SMALL, 528, [NT], f32)
        h0col = carve(SMALL, 616, [NT], f32)
        st6 = carve(SMALL, 704, [2, 6], f32)
        mv = carve(SMALL, 752, [2, 2], f32)
        veps = carve(SMALL, 768, [2, 1], f32)
        sd = carve(SMALL, 776, [2, 1], f32)
        rs = carve(SMALL, 784, [2, 1], f32)
        Fw = carve(SMALL, 792, [2, KT, 2 * H], f16)
        before = carve(SMALL, 1048, [NT + P], bf16)
        tri = carve(SMALL, 1348, [P], bf16)

        PS = ctx.enter_context(nc.psum_tensor("PS", [P, 8, D], f32))
        PSf = PS[:, :, :].rearrange("p a b -> p (a b)")
        spare = sb("spare", [P, 4], f32)
        small2 = sb("small2", [P, 352], f32)
        b_exp = carve(small2, 0, [H, NT], f32)
        d_neg = carve(small2, 704, [H, NT], f32)
        carry = carve(small2, 0, [2, P], bf16)

        block = ctx.enter_context(nc.Block())

        def everyone(eng, k):
            eng.drain().then_inc(S("phase"), 1)
            eng.wait_ge(S("phase"), 4 * k)

        SPLITS = [(0, 0, False), (1, 1, True), (2, 2, True), (3, 3, False), (4, 4, False)]
        MATS = {0: [0], 1: [1, 2], 2: [3, 4], 3: [5]}

        def rows(k):
            return P if k < NT - 1 else TAIL

        def parity_count(t, s):
            return 8 * (t - s) + 16

        def adj_count(t, s4):
            return 4 * (t - s4) + 16

        def unit(h2, hh, jt):
            return (2 * h2 + hh) * NT + jt

        def head_col(region, h2, hh, jt):
            return region[:, :, :].rearrange("p h t -> p (h t)")[:, bass.ds(unit(h2, hh, jt), 1)]

        def wh_tile(h2, hh, jt):
            return Yr[:, bass.ds(unit(h2, hh, jt) * OC, MC)]

        def heads(eng, work, before=None, after_first=None, at_end=None):
            def head(h2, hh):
                n = 2 * h2 + hh
                if before:
                    before(h2, hh)
                for jt in range(3):
                    if jt == 2 and after_first and inner(n, 1):
                        after_first(n - 1, 1 - hh)
                    work(h2, hh, jt, jt)
                with eng.Fori(3, NT - 3, 3) as j:
                    for k in range(3):
                        work(h2, hh, j + k, k)
                work(h2, hh, NT - 1, 1)
                if at_end and inner(n, 1):
                    at_end(n - 1, 1 - hh)
            head(0, 0)
            head(0, 1)
            with eng.Fori(1, H // 2, 1) as h2:
                head(h2, 0)
                head(h2, 1)
            if after_first:
                after_first(H - 1, 1)
            if at_end:
                at_end(H - 1, 1)

        def project_dve(dve, l):
            b0 = NT * l
            if l >= 2:
                dve.wait_ge(S("g_x"), NT * (l - 1))

            def rows_of(t, s):
                return stage[:, s, :] if l == 0 else X[:, t, :]

            def statistics(t, s):
                if l == 0:
                    dve.wait_ge(S(f"x{s}"), parity_count(t, s))
                if l == 1:
                    dve.wait_ge(S(f"xr{s}"), parity_count(t, s))
                    dve.scalar_tensor_tensor(tmpa[:, :], biasA[:, :], s_col[:, bass.ds(t, 1)], own0[:, t, :],
                                             ALU.mult, ALU.add).then_inc(S("p_t0"), 1)
                    dve.wait_ge(S("p_t0"), t + 1)
                    dve.scalar_tensor_tensor(X[:, t, :], tmpa[:, :], 0.0, X[:, t, :], ALU.max, ALU.add)\
                        .then_inc(S("p_x1"), 1)
                    dve.wait_ge(S("p_x1"), t + 1)
                dve.memset(spare[:, 0:1], 0.0)
                dve.bn_stats(st6[:, s, :], rows_of(t, s)).then_inc(S("p_st"), 1)
                dve.wait_ge(S("p_st"), b0 + t + 1)
                dve.memset(spare[:, 1:2], 0.0)
                dve.bn_aggr(mv[:, s, :], st6[:, s, :]).then_inc(S("p_mv"), 1)
                dve.wait_ge(S("p_mv"), b0 + t + 1)
                dve.tensor_scalar_add(veps[:, s, :], mv[:, s, 1:2], EPS).then_inc(S("p_var"), 1)

            def normalise_rows(t, s):
                dve.wait_ge(S("p_sd"), b0 + t + 1)
                dve.reciprocal(rs[:, s, :], sd[:, s, :]).then_inc(S("p_rs"), 1)
                dve.wait_ge(S("p_rs"), b0 + t + 1)
                dve.tensor_scalar(xn[:, s, :], rows_of(t, s), mv[:, s, 0:1], rs[:, s, :], ALU.subtract, ALU.mult)\
                    .then_inc(S("p_xn"), 1)
                if l == 0:
                    dve.wait_ge(S("p_xn"), t + 1)
                    dve.tensor_scalar(h0col[:, bass.ds(t, 1)], xn[:, s, 0:1], 0.0, 1.0 / H_SCALE, ALU.max, ALU.mult)\
                        .then_inc(S("p_h0"), 1)

            def low_part(t, s):
                dve.wait_ge(S("p_hi"), b0 + t + 1)
                if inner(t, 2):
                    dve.wait_ge(S("p_tr"), b0 + t - 1)
                dve.scalar_tensor_tensor(h_lo[:, s, :], xn[:, s, :], 0.0, h_hi[:, s, :], ALU.max, ALU.subtract)\
                    .then_inc(S("p_lo"), 1)

            def results(t, s):
                dve.wait_ge(S("p_mm"), b0 + t + 1)
                if l == 1:
                    if inner(t, 2):
                        dve.wait_ge(S(f"own_out{s}"), parity_count(t, s) - 16)
                    dve.scalar_tensor_tensor(stage[:, s, :], PS[:, 2 + s, :], UNSCALE, biasB[:, :],
                                             ALU.mult, ALU.add).then_inc(S("p_own"), 1)
                if l == 2:
                    if inner(t, 1):
                        dve.wait_ge(S("p_q3"), t)
                    dve.scalar_tensor_tensor(tmpa[:, :], PS[:, 2 + s, :], UNSCALE, biasA[:, :],
                                             ALU.mult, ALU.add).then_inc(S("p_q1"), 1)
                    dve.wait_ge(S("p_q1"), t + 1)
                    dve.scalar_tensor_tensor(tmpb[:, :], tmpa[:, :], 0.01, tmpa[:, :], ALU.mult, ALU.max)\
                        .then_inc(S("p_q2"), 1)
                    dve.wait_ge(S("p_q2"), t + 1)
                    dve.tensor_tensor(X[:, t, :], X[:, t, :], tmpb[:, :], ALU.add).then_inc(S("p_q3"), 1)
                dve.wait_ge(S("p_yhi"), b0 - NT + t + 1)
                dve.scalar_tensor_tensor(Y[:, t, 1, :], PS[:, 4 + s, :], Y_SCALE * UNSCALE, Y[:, t, 0, :],
                                         ALU.mult, ALU.subtract).then_inc(S("p_free"), 1)
            pipeline(dve, [(4, statistics), (3, normalise_rows), (2, low_part)] + ([(-1, results)] if l in (1, 2) else []))

        def project_act(act, l):
            b0 = NT * l

            def deviation(t, s):
                act.wait_ge(S("p_var"), b0 + t + 1)
                act.activation(sd[:, s, :], veps[:, s, :], ACT.Sqrt, scale=1.0 / H_SCALE ** 2).then_inc(S("p_sd"), 1)

            def high_part(t, s):
                act.wait_ge(S("p_xn"), b0 + t + 1)
                if inner(t, 2):
                    act.wait_ge(S("p_tr"), b0 + t - 1)
                act.activation(h_hi[:, s, :], xn[:, s, :], ACT.Relu).then_inc(S("p_hi"), 1)

            def transposed(t, s):
                act.wait_ge(S("p_tr"), b0 + t + 1)
                if inner(t, 2):
                    act.wait_ge(S("p_mm"), b0 + t - 1)
                act.activation(hT[:, s].rearrange("p a b -> p (a b)"), PS[:, s, :].bitcast(f16), ACT.Copy)\
                    .then_inc(S("p_hT"), 1)

            def results(t, s):
                act.wait_ge(S("p_mm"), b0 + t + 1)
                if l == 0:
                    act.activation(own0[:, t, :], PS[:, 2 + s, :], ACT.Copy, scale=UNSCALE).then_inc(S("p_free"), 1)
                elif l < 3:
                    act.activation(Y[:, t, 0, :], PS[:, 4 + s, :], ACT.Copy, scale=Y_SCALE * UNSCALE)\
                        .then_inc(S("p_yhi"), 1)
                else:
                    act.activation(Wh[:, :, t, 0:O], PS[:, 2 + s, :].rearrange("p (h o) -> p h o", o=O), ACT.Copy,
                                   scale=UNSCALE).then_inc(S("p_f"), 1)
                    act.activation(f1[:, :, bass.ds(t, 1)], PS[:, 4 + s, 0:H].unsqueeze(2), ACT.Copy,
                                   scale=UNSCALE).then_inc(S("p_f"), 1)
                    act.activation(f2[:, :, bass.ds(t, 1)], PS[:, 4 + s, H:2 * H].unsqueeze(2), ACT.Copy,
                                   scale=UNSCALE).then_inc(S("p_free"), 1)
            pipeline(act, [(4, deviation), (3, high_part), (1, transposed), (-1, results)])

        def project_pe(pe, l):
            b0 = NT * l
            pe.wait_ge(S("wt"), 16 * sum(len(MATS[k]) for k in range(l + 1)))
            if l == 3:
                pe.wait_ge(S("fw_lo"), 1)

            def turn(t, s):
                pe.wait_ge(S("p_lo"), b0 + t + 1)
                if inner(t, 2):
                    pe.wait_ge(S("p_hT"), b0 + t - 1)
                for part, h in enumerate((h_hi, h_lo)):
                    for k in range(KT):
                        c = part * KT + k
                        ins = pe.transpose(PS[:, s, :].bitcast(f16)[:, c * P:(c + 1) * P],
                                           h[:, s, k * P:(k + 1) * P], ident_h[:, :])
                ins.then_inc(S("p_tr"), 1)

            def products(t, s):
                pe.wait_ge(S("p_hT"), b0 + t + 1)
                if inner(t, 2):
                    pe.wait_ge(S("p_free"), b0 + t - 1)
                outs = [(PS[:, 2 + s, :], lambda part, k: Wt[:, 0, part, k, :])]
                if l in (1, 2):
                    outs.append((PS[:, 4 + s, :], lambda part, k: Wt[:, 1, part, k, :]))
                if l == 3:
                    outs.append((PS[:, 4 + s, 0:2 * H], lambda part, k: Fw[:, part, k, :]))
                for hpart, wparts in ((0, (0, 1)), (1, (0,))):
                    for k in range(KT):
                        for dst, w in outs:
                            for wpart in wparts:
                                ins = pe.matmul(dst, hT[:, s, hpart * KT + k, :], w(wpart, k),
                                                start=hpart == 0 and k == 0 and wpart == 0,
                                                stop=hpart == 1 and k == KT - 1)
                ins.then_inc(S("p_mm"), 1)
            pipeline(pe, [(2, turn), (0, products)])

        def aggregate_dve(dve, l):
            b0 = NT * (l - 1)

            def neighbours(t, s):
                if inner(t, 2):
                    dve.wait_ge(S("g_mm"), b0 + t - 1)
                dve.tensor_scalar(blk[:, s], V[:, :, bass.ts(t, P)], 2.0, None,
                                  ALU.is_ge if l == 1 else ALU.is_equal).then_inc(S("g_blk"), 1)
                if l == 2:
                    dve.tensor_scalar(V[:, :, bass.ts(t, P)], V[:, :, bass.ts(t, P)], 2.0, None, ALU.is_ge)\
                        .then_inc(S("g_v"), 1)

            def update(t, s):
                dve.wait_ge(S("g_mm"), b0 + t + 1)
                if inner(t, 1):
                    dve.wait_ge(S("g_x"), b0 + t)
                if l == 1:
                    dve.wait_ge(S(f"own_in{s}"), parity_count(t, s))
                    dve.scalar_tensor_tensor(tmpa[:, :], PS[:, 6 + s, :], rdeg[:, bass.ds(t, 1)], stage[:, s, :],
                                             ALU.mult, ALU.add).then_inc(S("g_t1"), 1)
                    dve.wait_ge(S("g_t1"), b0 + t + 1)
                    dve.scalar_tensor_tensor(X[:, t, :], tmpa[:, :], 0.0, X[:, t, :], ALU.max, ALU.add)\
                        .then_inc(S("g_x"), 1)
                else:
                    dve.scalar_tensor_tensor(tmpa[:, :], PS[:, 6 + s, :], rcnt[:, bass.ds(t, 1)], biasC[:, :],
                                             ALU.mult, ALU.add).then_inc(S("g_t1"), 1)
                    dve.wait_ge(S("g_t1"), b0 + t + 1)
                    dve.scalar_tensor_tensor(tmpb[:, :], tmpa[:, :], 0.01, tmpa[:, :], ALU.mult, ALU.max)\
                        .then_inc(S("g_t2"), 1)
                    dve.wait_ge(S("g_t2"), t + 1)
                    dve.scalar_tensor_tensor(X[:, t, :], tmpb[:, :], has[:, bass.ds(t, 1)], X[:, t, :],
                                             ALU.mult, ALU.add).then_inc(S("g_x"), 1)
            if l == 2:
                dve.wait_ge(S("p_q3"), NT)
            pipeline(dve, [(1, neighbours), (-1, update)])

        def aggregate_pe(pe, l):
            b0 = NT * (l - 1)
            pe.wait_ge(S("p_free"), NT * (l + 1))

            def aggregate(t, s):
                pe.wait_ge(S("g_blk"), b0 + t + 1)
                if inner(t, 2):
                    pe.wait_ge(S("g_t1"), b0 + t - 1)
                for j in range(NT):
                    for part in range(2):
                        ins = pe.matmul(PS[:, 6 + s, :], blk[:, s, j, :], Y[:, j, part, :],
                                        start=j == 0 and part == 0, stop=j == NT - 1 and part == 1)
                ins.then_inc(S("g_mm"), 1)
            pipeline(pe, [(0, aggregate)])

        @block.sync
        def _(sp):
            by_rows = "(t p) k -> p t k"
            sp.dma_start(raw[:, 0], w_self0.rearrange(by_rows, p=P)).then_inc(S("raw0"), 16)
            sp.dma_start(raw[:, 1], w_self1.rearrange(by_rows, p=P)).then_inc(S("raw1"), 16)
            sp.dma_start(wc[:, 0], w_comb[0:D, :].rearrange(by_rows, p=P)).then_inc(S("wc0"), 16)
            with nc.allow_non_contiguous_dma(reason="biases as columns"):
                sp.dma_start(bcol[:, 0, :], b_self1.rearrange("(t p) -> p t", p=P)).then_inc(S("bcol"), 16)
                sp.dma_start(bcol[:, 1, :], b_nb1.rearrange("(t p) -> p t", p=P)).then_inc(S("bcol"), 16)
            sp.dma_start(raw[:, 2], w_nb1.rearrange(by_rows, p=P)).then_inc(S("raw2"), 16)
            sp.dma_start(wc[:, 1], w_comb[D:2 * D, :].rearrange(by_rows, p=P)).then_inc(S("wc1"), 16)
            sp.dma_start(biasB[:, :], b_comb.partition_broadcast(P)).then_inc(S("biasB"), 16)
            sp.dma_start(raw[:, 3], w_line2.rearrange(by_rows, p=P)).then_inc(S("raw3"), 16)
            sp.dma_start(raw[:, 4], w_nb2.rearrange(by_rows, p=P)).then_inc(S("raw4"), 16)
            sp.dma_start(a12[:, 0, :], a1.rearrange("h o -> (h o)").partition_broadcast(P)).then_inc(S("a12"), 16)
            sp.dma_start(a12[:, 1, :], a2.rearrange("h o -> (h o)").partition_broadcast(P)).then_inc(S("a12"), 16)
            sp.wait_ge(S("w_tr"), KT)
            sp.dma_start(raw[:, 0], w_neigh0.rearrange(by_rows, p=P)).then_inc(S("raw0"), 16)
            sp.wait_ge(S("w_tr"), 2 * KT)
            for k in range(KT):
                sp.dma_start(raw[:, 1, k, :].rearrange("p (h o) -> p h o", o=O),
                             w3[:, k * P:(k + 1) * P, :].rearrange("h p o -> p h o")).then_inc(S("raw1"), 16)

            def store_parts(m):
                sp.wait_ge(S("w_lo"), m + 1)
                sp.dma_start(w_parts[m], parts[m % 2].rearrange("p a b c -> p (a b c)")).then_inc(S(f"w_out{m % 2}"), 16)
            for m in range(6):
                store_parts(m)
                if m == 1:
                    for t in range(4):
                        sp.dma_start(adj_in[:, t, :], adj[t * P:(t + 1) * P, :]).then_inc(S(f"adj{t}"), 16)
            sp.wait_ge(S("w_out0"), 48)
            sp.wait_ge(S("w_out1"), 48)

            def load_weights(layer):
                for n, m in enumerate(MATS[layer]):
                    sp.dma_start(Wt[:, n].rearrange("p a b c -> p (a b c)"), w_parts[m]).then_inc(S("wt"), 16)
            load_weights(0)

            def load_x(t, s):
                if inner(t, 2):
                    sp.wait_ge(S("p_xn"), t - 1)
                if isinstance(t, int) and t == NT - 1:
                    sp.dma_start(stage[0:TAIL, s, :], x_in[t * P:N, :]).then_inc(S(f"x{s}"), 16)
                else:
                    sp.dma_start(stage[:, s, :], x_in[bass.ts(t, P), :]).then_inc(S(f"x{s}"), 16)
            pipeline(sp, [(0, load_x)])

            sp.wait_ge(S("h0_sb"), 1)
            sp.dma_start(h0_row[:, :], rT[0:NT, 0, :]).then_inc(S("h0_dram"), 16)
            sp.wait_ge(S("h0_dram"), 16)
            sp.wait_ge(S("phase"), 4)
            sp.dma_start(h0_all[:, :], h0_row.rearrange("a b -> (a b)").partition_broadcast(P)).then_inc(S("h0_all"), 16)

            def load_adj(t, s):
                if isinstance(t, int) and t < 4:
                    return
                sp.wait_ge(S("b_mask"), t - 3)
                sp.wait_ge(S("b_rowsum"), t - 3)
                sp.wait_ge(S("b_s"), t - 3)
                if isinstance(t, int) and t == NT - 1:
                    sp.dma_start(adj_in[0:TAIL, s, :], adj[t * P:N, :]).then_inc(S(f"adj{s}"), 16)
                else:
                    sp.dma_start(adj_in[:, s, :], adj[bass.ts(t, P), :]).then_inc(S(f"adj{s}"), 16)
            pipeline(sp, [(0, load_adj)], period=4)

            sp.wait_ge(S("phase"), 8)
            load_weights(1)
            sp.wait_ge(S("x_clear"), 1)

            def load_x1(t, s):
                if inner(t, 2):
                    sp.wait_ge(S("p_x1"), t - 1)
                if isinstance(t, int) and t == NT - 1:
                    sp.dma_start(X[0:TAIL, t, :], x_in[t * P:N, :]).then_inc(S(f"xr{s}"), 16)
                else:
                    sp.dma_start(X[:, t, :], x_in[bass.ts(t, P), :]).then_inc(S(f"xr{s}"), 16)

            def store_own(t, s):
                sp.wait_ge(S("p_own"), t + 1)
                sp.dma_start(self_rows[t], stage[:, s, :]).then_inc(S(f"own_out{s}"), 16)
            pipeline(sp, [(6, load_x1), (-1, store_own)])
            for s in range(2):
                sp.wait_ge(S(f"own_out{s}"), 16 * (NT // 2))

            def load_own(t, s):
                if inner(t, 2):
                    sp.wait_ge(S("g_t1"), t - 1)
                sp.dma_start(stage[:, s, :], self_rows[t]).then_inc(S(f"own_in{s}"), 16)
            sp.wait_ge(S("p_mm"), 2 * NT)
            load_weights(2)
            pipeline(sp, [(0, load_own)])
            sp.wait_ge(S("phase"), 12)
            sp.dma_start(biasA[:, :], b_line2.partition_broadcast(P)).then_inc(S("bias2"), 16)
            sp.dma_start(biasC[:, :], b_nb2.partition_broadcast(P)).then_inc(S("bias2"), 16)
            sp.wait_ge(S("p_mm"), 3 * NT)
            load_weights(3)

            sp.wait_ge(S("r_sb"), 2)
            sp.dma_start(ratio_rows[0:P, :], rT[:, 0, :]).then_inc(S("r_dram"), 16)
            sp.dma_start(ratio_rows[P:H * NT, :], rT[0:H * NT - P, 1, :]).then_inc(S("r_dram"), 16)
            sp.wait_ge(S("r_dram"), 32)
            sp.wait_ge(S("phase"), 16)
            for h in range(H):
                if h >= 2:
                    sp.wait_ge(S("l_relu"), NT * (h - 1))
                sp.dma_start(ratio[h % 2][:, :], ratio_flat[h * NP:(h + 1) * NP].partition_broadcast(P))\
                  .then_inc(S(f"ratio{h % 2}"), 16)
            for t in range(NT):
                sp.wait_ge(S("l_out"), 1)
                sp.dma_start(out[t * P:t * P + rows(t), :], X[0:rows(t), t, :]).then_inc(S("out"), 16)
            sp.wait_ge(S("out"), 16 * NT)

        @block.gpsimd
        def _(pool):
            for m in (ident_f, ident_h, ident_b):
                pool.memset(m[:, :], 0.0).then_inc(S("zeroed"), 1)
            pool.wait_ge(S("zeroed"), 3)
            for m in (ident_f, ident_h, ident_b):
                pool.affine_select(out=m[:, :], in_=m[:, :], compare_op=ALU.not_equal, fill=1.0,
                                   base=0, pattern=[[-1, P]], channel_multiplier=1).then_inc(S("ident"), 1)
            everyone(pool, 1)
            pool.memset(mask[:, :, N:NP], 0.0).then_inc(S("cst0"), 1)
            pool.memset(before[:, 0:NT], 0.0).then_inc(S("cst0"), 1)
            pool.memset(before[:, NT:NT + P], 1.0 / EDGE).then_inc(S("cst0"), 1)
            pool.memset(tri[:, 0:P], 1.0 / EDGE).then_inc(S("cst0"), 1)
            pool.memset(pick[:, :, :], 0.0).then_inc(S("cst0"), 1)
            pool.wait_ge(S("cst0"), 5)
            pool.affine_select(out=tri[:, 0:P], in_=tri[:, 0:P], compare_op=ALU.is_ge, fill=0.0,
                               base=0, pattern=[[1, P]], channel_multiplier=-1).then_inc(S("cst"), 1)
            pool.affine_select(out=pick[:, :, :], in_=pick[:, :, :], compare_op=ALU.not_equal, fill=1.0,
                               base=0, pattern=[[-1, NT], [0, P]], channel_multiplier=1).then_inc(S("cst"), 1)

            everyone(pool, 2)
            everyone(pool, 3)
            pool.wait_ge(S("fmax"), 2)
            pool.partition_all_reduce(gmax[:, :, :].rearrange("p a b -> p (a b)"),
                                      fmax[:, :, :].rearrange("p a b -> p (a b)"), P, RMAX).then_inc(S("gmax"), 1)
            everyone(pool, 4)

        @block.scalar
        def _(act):
            ev = 0
            pv = 0
            for job, m, product in SPLITS:
                for k in range(KT):
                    act.wait_ge(S("w_tr"), ev + 1)
                    if k == 0 and job >= 2:
                        act.wait_ge(S("w_lo"), job - 1)
                    act.activation(wT[:, job % 2, k, :], PS[:, ev % 2, :], ACT.Copy).then_inc(S("w_ev"), 1)
                    ev += 1
                src = wT[:, job % 2]
                if product:
                    for k in range(KT):
                        act.wait_ge(S("w_mm"), pv + 1)
                        if k == 0 and pv:
                            act.wait_ge(S("w_lo"), m)
                        act.activation(wP[:, k, :], PS[:, 2 + pv % 2, :], ACT.Copy).then_inc(S("w_pev"), 1)
                        pv += 1
                    src = wP
                    act.wait_ge(S("w_pev"), pv)
                else:
                    act.wait_ge(S("w_ev"), ev)
                if m >= 2:
                    act.wait_ge(S(f"w_out{m % 2}"), 16 * (m // 2))
                act.activation(parts[m % 2][:, 0], src, ACT.Copy, scale=W_SCALE).then_inc(S("w_hi"), 1)
            act.wait_ge(S("wsum_ps"), 1)
            act.activation(biasA[:, :], PS[:, 6, :], ACT.Copy).then_inc(S("wsum"), 1)
            act.wait_ge(S("raw1"), 16 + 16 * KT)
            act.wait_ge(S("w_out1"), 32)
            act.activation(parts[1][:, 0], raw[:, 1], ACT.Copy, scale=W_SCALE).then_inc(S("w_hi"), 1)
            act.wait_ge(S("fw32"), 1)
            act.activation(Fw[:, 0], fw32[:, :, :], ACT.Copy, scale=W_SCALE).then_inc(S("fw_hi"), 1)

            project_act(act, 0)
            act.wait_ge(S("h0_ps"), 1)
            act.activation(rT[0:NT, 0, :], PS[0:NT, 0, 0:P], ACT.Copy).then_inc(S("h0_sb"), 1)
            everyone(act, 1)

            def row_sum(t, s4):
                act.wait_ge(S(f"adj{s4}"), adj_count(t, s4))
                if inner(t, 1):
                    act.wait_ge(S("b_rowsum"), t)
                act.activation(junk_s[:, 0:N], adj_in[:, s4, :], ACT.Copy,
                               accum_out=rowsum[:, bass.ds(t, 1)]).then_inc(S("b_rowsum"), 1)

            def mask_out(t, s4):
                s = s4 % 2
                for g in range(3):
                    n = min(8, NT - 8 * g)
                    act.wait_ge(S("b_tr"), 3 * t + g + 1)
                    if g == 0 and inner(t, 2):
                        act.wait_ge(S("b_code"), 3 * t - 3)
                    act.activation(maskT[:, s, 8 * g:8 * g + n, :].rearrange("p a b -> p (a b)"),
                                   PS[:, g, :].bitcast(bf16)[:, 0:n * P], ACT.Copy, scale=EDGE).then_inc(S("b_maskT"), 1)
            pipeline(act, [(2, row_sum), (1, mask_out)], period=4)
            everyone(act, 2)

            project_act(act, 1)
            everyone(act, 3)
            project_act(act, 2)
            project_act(act, 3)
            act.wait_ge(S("args"), 1)
            act.activation(rexp[:, :, :], rarg[:, :, :], ACT.Exp).then_inc(S("exps"), 1)
            act.activation(b_exp[:, :, :], barg[:, :, :], ACT.Exp).then_inc(S("exps"), 1)
            act.activation(dexp[:, :, :], darg[:, :, :], ACT.Exp).then_inc(S("exps"), 1)
            for k in range(2):
                n = P if k == 0 else H * NT - P
                act.wait_ge(S("r_ps"), k + 1)
                act.activation(rT[0:n, k, :], PS[0:n, k, 0:P], ACT.Copy).then_inc(S("r_sb"), 1)
            act.wait_ge(S("mean_lo"), 1)
            act.activation(mean_lo[:, :], mean_lo[:, :], ACT.Exp).then_inc(S("mean_exp"), 1)
            everyone(act, 4)

            def relu(h2, hh, jt, slot):
                act.wait_ge(S("prob_free"), unit(h2, hh, jt) + (2 if isinstance(jt, int) and jt in (1, NT - 1) else 1))
                act.activation(prob[slot][:, :], ratio[hh][:, :], ACT.Relu,
                               bias=head_col(d_neg, h2, hh, jt), scale=head_col(b_exp, h2, hh, jt)).then_inc(S("l_relu"), 1)

            def elu_exp(n, k):
                act.wait_ge(S("l_min"), n + 1)
                slab = Wh[:, n, :, 0:O]
                act.activation(slab, slab, ACT.Exp).then_inc(S("l_exp"), 1)
            heads(act, relu, at_end=elu_exp,
                  before=lambda h2, hh: act.wait_ge(S(f"ratio{hh}"), 16 * h2 + 16))

        @block.vector
        def _(dve):
            links = [0]

            def link(ins):
                links[0] += 1
                ins.then_inc(S("link"), 1)
                dve.wait_ge(S("link"), links[0])

            dve.wait_ge(S("bcol"), 32)
            dve.tensor_copy(bcols[:, :, :], bcol[:, 0, :].unsqueeze(2).to_broadcast([P, KT, P])).then_inc(S("bcols"), 1)

            def low(m, src):
                dve.wait_ge(S("w_hi"), m + 1)
                dve.scalar_tensor_tensor(parts[m % 2][:, 1].rearrange("p a b -> p (a b)"), src.rearrange("p a b -> p (a b)"),
                                         W_SCALE, parts[m % 2][:, 0].rearrange("p a b -> p (a b)"),
                                         ALU.mult, ALU.subtract).then_inc(S("w_lo"), 1)
            low(0, wT[:, 0])
            dve.wait_ge(S("w_bias"), 1)
            dve.tensor_copy(bcols[:, :, :], bcol[:, 1, :].unsqueeze(2).to_broadcast([P, KT, P])).then_inc(S("bcols"), 1)
            low(1, wP)
            low(2, wP)
            dve.wait_ge(S("w_bias"), 2)
            dve.wait_ge(S("biasB"), 16)
            dve.scalar_tensor_tensor(biasB[:, :], PS[:, 7, :], 1.0, biasB[:, :], ALU.mult, ALU.add).then_inc(S("bias1"), 1)
            low(3, wT[:, 1])
            low(4, wT[:, 0])
            dve.wait_ge(S("raw0"), 32)
            link(dve.tensor_reduce(rsum4[:, :], raw[:, 0], AX.X, ALU.add))
            dve.tensor_copy(rcols[:, :, :], rsum4[:, :].unsqueeze(2).to_broadcast([P, KT, P])).then_inc(S("rcols"), 1)
            low(5, raw[:, 1])
            dve.wait_ge(S("a12"), 32)
            for a in range(2):
                for k in range(KT):
                    link(dve.tensor_tensor(wP[:, 2, :], raw[:, 1, k, :], a12[:, a, :], ALU.mult))
                    link(dve.tensor_reduce(fw32[:, k, a * H:(a + 1) * H],
                                           wP[:, 2, :].rearrange("p (h o) -> p h o", o=O), AX.X, ALU.add))
            dve.sem_inc(S("fw32"), 1)
            dve.wait_ge(S("fw_hi"), 1)
            dve.scalar_tensor_tensor(Fw[:, 1], fw32[:, :, :], W_SCALE, Fw[:, 0], ALU.mult, ALU.subtract)\
                .then_inc(S("fw_lo"), 1)

            project_dve(dve, 0)
            everyone(dve, 1)

            dve.wait_ge(S("h0_all"), 16)

            def neighbour_sum(t, s4):
                dve.wait_ge(S(f"adj{s4}"), adj_count(t, s4))
                if inner(t, 1):
                    dve.wait_ge(S("b_s"), t)
                dve.scalar_tensor_tensor(junk_v[:, 0:N], adj_in[:, s4, :], 1.0, h0_all[:, 0:N], ALU.mult, ALU.mult,
                                         accum_out=s_col[:, bass.ds(t, 1)]).then_inc(S("b_s"), 1)

            def make_mask(t, s4):
                s = s4 % 2
                if inner(t, 2):
                    dve.wait_ge(S("b_tr"), 3 * t - 3)
                dve.tensor_scalar(mask[:, s, 0:N], adj_in[:, s4, :], 0.0, None, ALU.is_gt).then_inc(S("b_mask"), 1)

            def counts_out(t, s4):
                dve.wait_ge(S("b_count"), t + 1)
                dve.tensor_copy(deg[:, bass.ds(t, 1)], PS[:, 7, P:P + 1])
                dve.tensor_scalar_min(carry[:, s4 % 2, :], PS[:, 7, 0:P], KEEP + 1.0).then_inc(S("b_carry"), 1)

            def code_out(t, s4):
                s = s4 % 2
                for g in range(3):
                    n = min(8, NT - 8 * g)
                    b = 3 + 2 * ((s + g) % 2)
                    dve.wait_ge(S("b_cum"), 3 * t + g + 1)
                    dve.scalar_tensor_tensor(
                        V[:, 8 * g:8 * g + n, bass.ts(t, P)],
                        PSf[:, b * D:b * D + n * P].rearrange("p (a b) -> p a b", b=P),
                        KEEP + 0.5, maskT[:, s, 8 * g:8 * g + n, :], ALU.is_gt, ALU.add)\
                        .then_inc(S("b_code"), 1)
            pipeline(dve, [(2, neighbour_sum), (2, make_mask), (0, counts_out), (0, code_out)], period=4)
            dve.wait_ge(S("b_rowsum"), NT)
            dve.wait_ge(S("b_s"), NT)
            dve.wait_ge(S("b_carry"), NT)
            link(dve.scalar_tensor_tensor(s_col[:, :], rowsum[:, :], 0.0, s_col[:, :], ALU.is_gt, ALU.mult))
            link(dve.tensor_scalar(rdeg[:, :], deg[:, :], 1.0, Y_SCALE, ALU.max, ALU.mult))
            link(dve.reciprocal(rdeg[:, :], rdeg[:, :]))
            link(dve.tensor_scalar(rcnt[:, :], deg[:, :], float(KEEP), 1.0, ALU.min, ALU.max))
            link(dve.tensor_scalar(rcnt[:, :], rcnt[:, :], Y_SCALE, None, ALU.mult))
            link(dve.reciprocal(rcnt[:, :], rcnt[:, :]))
            link(dve.tensor_scalar(has[:, :], deg[:, :], 0.0, None, ALU.is_gt))
            link(dve.tensor_scalar(iso[:, :], has[:, :], -1.0, 1.0, ALU.mult, ALU.add))
            everyone(dve, 2)
            dve.memset(X[:, NT - 1, :], 0.0).then_inc(S("x_clear"), 1)

            project_dve(dve, 1)
            aggregate_dve(dve, 1)
            everyone(dve, 3)
            dve.wait_ge(S("bias2"), 32)
            project_dve(dve, 2)
            aggregate_dve(dve, 2)
            link(dve.memset(Wh[:, :, :, O:OC], 1.0))
            link(dve.memset(Yr[:, NT * H * OC:NT * H * OC + MC - OC], 0.0))
            link(dve.memset(ones_f[:, :], 1.0))
            project_dve(dve, 3)

            dve.wait_ge(S("p_free"), 4 * NT)
            for k, f in enumerate((f1, f2)):
                dve.tensor_reduce(fmax[:, k, :], f[:, :, :], AX.X, ALU.max).then_inc(S("fmax"), 1)
            dve.wait_ge(S("gmax"), 1)
            link(dve.tensor_tensor(zmax[:, :], gmax[:, 0, :], gmax[:, 1, :], ALU.add))
            link(dve.tensor_scalar(guard[:, :], zmax[:, :], 0.8, 0.0, ALU.mult, ALU.max))
            link(dve.tensor_scalar(guard[:, :], guard[:, :], -1.0, 60.0, ALU.mult, ALU.add))
            link(dve.scalar_tensor_tensor(rbias[:, :], gmax[:, 1, :], 0.8, guard[:, :], ALU.mult, ALU.add))
            link(dve.scalar_tensor_tensor(rarg[:, :, :], f1[:, :, :], 0.8,
                                          rbias[:, :].unsqueeze(2).to_broadcast([P, H, NT]), ALU.mult, ALU.add))
            link(dve.tensor_tensor(barg[:, :, :], f2[:, :, :],
                                   gmax[:, 1, :].unsqueeze(2).to_broadcast([P, H, NT]), ALU.subtract))
            link(dve.scalar_tensor_tensor(darg[:, :, :], barg[:, :, :], 0.2,
                                          guard[:, :].unsqueeze(2).to_broadcast([P, H, NT]), ALU.mult, ALU.add))
            dve.sem_inc(S("args"), 1)
            dve.wait_ge(S("exps"), 3)
            link(dve.tensor_scalar(d_neg[:, :, :], dexp[:, :, :], -1.0, None, ALU.mult))
            dve.wait_ge(S("mean_ps"), 1)
            dve.tensor_scalar(mean_hi[:, :], PS[:, 2, :], 1.0 / N, 0.0, ALU.mult, ALU.max).then_inc(S("mean_hi"), 1)
            dve.tensor_scalar(mean_lo[:, :], PS[:, 2, :], 1.0 / N, 0.0, ALU.mult, ALU.min).then_inc(S("mean_lo"), 1)
            dve.wait_ge(S("mean_exp"), 1)
            dve.wait_ge(S("mean_hi"), 1)
            link(dve.scalar_tensor_tensor(mean_lo[:, :], mean_lo[:, :], -1.0, mean_hi[:, :], ALU.add, ALU.add))
            for t in range(NT):
                dve.scalar_tensor_tensor(X[:, t, :], mean_lo[:, :], iso[:, t:t + 1], X[:, t, :],
                                         ALU.mult, ALU.add).then_inc(S("x_iso"), 1)
            dve.wait_ge(S("x_iso"), NT)
            everyone(dve, 4)

            def masked(h2, hh, jt, slot):
                dve.wait_ge(S("l_relu"), unit(h2, hh, jt) + 1)
                dve.scalar_tensor_tensor(prob[slot][:, :], prob[slot][:, :], head_col(d_neg, h2, hh, jt),
                                         V[:, jt, :], ALU.subtract, ALU.mult).then_inc(S("l_prob"), 1)

            def normalise(n, k):
                dve.wait_ge(S("prob_free"), NT * (n + 1) + 3)
                for b in range(NB):
                    g = min(PB, NT - PB * b)
                    sums = PS[:, b, 0:g * MC].rearrange("p (a c) -> p a c", c=MC)
                    dve.tensor_scalar(h0col[:, PB * b:PB * b + g].unsqueeze(2), sums[:, :, O:OC], 1e-37, None,
                                      ALU.max).then_inc(S("l_den"), 1)
                dve.wait_ge(S("l_den"), NB * (n + 1))
                dve.reciprocal(h0col[:, :], h0col[:, :]).then_inc(S("l_rden"), 1)
                dve.wait_ge(S("l_rden"), n + 1)
                for b in range(NB):
                    g = min(PB, NT - PB * b)
                    sums = PS[:, b, 0:g * MC].rearrange("p (a c) -> p a c", c=MC)
                    dve.tensor_tensor(Wh[:, n, PB * b:PB * b + g, 0:O], sums[:, :, 0:O],
                                      h0col[:, PB * b:PB * b + g].unsqueeze(2).to_broadcast([P, g, O]),
                                      ALU.mult).then_inc(S("l_norm"), 1)
                dve.wait_ge(S("l_norm"), NB * (n + 1))
                slab = Wh[:, n, :, 0:O]
                xh = X[:, :, bass.ts(n, O)]
                dve.scalar_tensor_tensor(xh, slab, 0.0, xh, ALU.max, ALU.add).then_inc(S("l_pos"), 1)
                dve.tensor_scalar(slab, slab, 0.0, None, ALU.min).then_inc(S("l_min"), 1)

            def finish(n, k):
                dve.wait_ge(S("l_exp"), n + 1)
                dve.wait_ge(S("l_pos"), n + 1)
                xh = X[:, :, bass.ts(n, O)]
                dve.scalar_tensor_tensor(xh, Wh[:, n, :, 0:O], -1.0, xh, ALU.add, ALU.add).then_inc(S("l_x"), 1)
            heads(dve, masked, after_first=normalise, at_end=finish)
            dve.wait_ge(S("l_x"), H)
            dve.sem_inc(S("l_out"), 1)

        @block.tensor
        def _(pe):
            pe.wait_ge(S("ident"), 3)
            n = 0
            q = 0
            for job, m, product in SPLITS:
                pe.wait_ge(S(f"raw{job}"), 16)
                for k in range(KT):
                    if n >= 2:
                        pe.wait_ge(S("w_ev"), n - 1)
                    for o in range(KT):
                        ins = pe.transpose(PS[:, n % 2, o * P:(o + 1) * P], raw[:, job, o, k * P:(k + 1) * P],
                                           ident_f[:, :])
                    ins.then_inc(S("w_tr"), 1)
                    n += 1
                if product:
                    pe.wait_ge(S("w_ev"), n)
                    pe.wait_ge(S(f"wc{m - 1}"), 16)
                    for k in range(KT):
                        if q >= 2:
                            pe.wait_ge(S("w_pev"), q - 1)
                        for c in range(KT):
                            ins = pe.matmul(PS[:, 2 + q % 2, :], wT[:, job % 2, c, k * P:(k + 1) * P], wc[:, m - 1, c, :],
                                            start=c == 0, stop=c == KT - 1)
                        ins.then_inc(S("w_mm"), 1)
                        q += 1
                    pe.wait_ge(S("bcols"), m)
                    for c in range(KT):
                        ins = pe.matmul(PS[:, 7, :], bcols[:, c, :], wc[:, m - 1, c, :],
                                        start=m == 1 and c == 0, stop=m == 2 and c == KT - 1)
                    ins.then_inc(S("w_bias"), 1)
            pe.wait_ge(S("rcols"), 1)
            for c in range(KT):
                ins = pe.transpose(PS[:, 6, c * P:(c + 1) * P], rcols[:, c, :], ident_f[:, :])
            ins.then_inc(S("wsum_ps"), 1)

            project_pe(pe, 0)
            pe.wait_ge(S("p_h0"), NT)
            pe.transpose(PS[0:NT, 0, 0:P], h0col[:, :], ident_f[:, :]).then_inc(S("h0_ps"), 1)
            everyone(pe, 1)
            pe.wait_ge(S("cst"), 2)

            def mask_turn(t, s4):
                s = s4 % 2
                pe.wait_ge(S("b_mask"), t + 1)
                for g in range(3):
                    if inner(t, 1):
                        pe.wait_ge(S("b_maskT"), 3 * t - 2 + g)
                    for c in range(min(8, NT - 8 * g)):
                        j = 8 * g + c
                        ins = pe.transpose(PS[:, g, :].bitcast(bf16)[:, c * P:(c + 1) * P],
                                           mask[:, s, j * P:(j + 1) * P], ident_b[:, :])
                    ins.then_inc(S("b_tr"), 1)

            def tile_counts(t, s4):
                s = s4 % 2
                pe.wait_ge(S("b_maskT"), 3 * t + 3)
                if inner(t, 1):
                    pe.wait_ge(S("b_carry"), t)
                for j in range(NT):
                    pe.matmul(PS[:, 7, 0:P], before[:, NT - 1 - j:NT - 1 - j + P], maskT[:, s, j, :],
                              start=j == 0, stop=j == NT - 1)
                for j in range(NT):
                    ins = pe.matmul(PS[:, 7, P:P + 1], maskT[:, s, j, :], before[:, NT:NT + 1],
                                    start=j == 0, stop=j == NT - 1)
                ins.then_inc(S("b_count"), 1)

            def running(t, s4):
                s = s4 % 2
                pe.wait_ge(S("b_carry"), t + 1)
                for g in range(3):
                    n = min(8, NT - 8 * g)
                    b = 3 + 2 * ((s + g) % 2)
                    if not (isinstance(t, int) and 3 * t + g < 2):
                        pe.wait_ge(S("b_code"), 3 * t + g - 1)
                    for half in range((n + 3) // 4):
                        m = min(4, n - 4 * half)
                        j0 = 8 * g + 4 * half
                        pe.matmul(PS[:, b + half, 0:m * P], tri[:, 0:P], maskT[:, s, j0:j0 + m, :],
                                  start=True, stop=False, skip_group_check=True)
                        for c in range(m):
                            ins = pe.matmul(PS[:, b + half, c * P:(c + 1) * P], pick[:, j0 + c, :], carry[:, s, :],
                                            start=False, stop=c == m - 1, skip_group_check=True)
                    ins.then_inc(S("b_cum"), 1)
            pipeline(pe, [(1, mask_turn), (0, tile_counts), (0, running)], period=4)
            everyone(pe, 2)

            project_pe(pe, 1)
            aggregate_pe(pe, 1)
            everyone(pe, 3)
            project_pe(pe, 2)
            aggregate_pe(pe, 2)
            project_pe(pe, 3)
            pe.wait_ge(S("exps"), 1)
            rflat = rexp[:, :, :].rearrange("p a b -> p (a b)")
            pe.transpose(PS[:, 0, 0:P], rflat[:, 0:P], ident_f[:, :]).then_inc(S("r_ps"), 1)
            pe.transpose(PS[0:H * NT - P, 1, 0:P], rflat[:, P:H * NT], ident_f[:, :]).then_inc(S("r_ps"), 1)
            for t in range(NT):
                r = rows(t)
                ins = pe.matmul(PS[:, 2, :].rearrange("p (h o) -> p h o", o=O), ones_f[0:r, :], Wh[0:r, :, t, 0:O],
                                start=t == 0, stop=t == NT - 1)
            ins.then_inc(S("mean_ps"), 1)
            pe.sem_inc(S("prob_free"), 3)
            everyone(pe, 4)

            def attend(h2, hh, jt, slot):
                pe.wait_ge(S("l_prob"), unit(h2, hh, jt) + 1)
                for i in range(NT):
                    b, c = i // PB, (i % PB) * MC
                    first = isinstance(jt, int) and jt == 0 and c == 0
                    if first and (not isinstance(h2, int) or 2 * h2 + hh >= 1):
                        pe.wait_ge(S("l_norm"), NB * (2 * h2 + hh - 1) + b + 1)
                    ins = pe.matmul(PS[:, b, c:c + MC], prob[slot][:, i * P:(i + 1) * P], wh_tile(h2, hh, jt),
                                    start=first, stop=False, skip_group_check=True)
                ins.then_inc(S("prob_free"), 1)

            heads(pe, attend)


_INS = ["x", "adj", "L0_gnn_w_self", "L0_gnn_w_neigh", "L1_gnn_W_self", "L1_gnn_b_self", "L1_gnn_W_nb",
        "L1_gnn_b_nb", "L1_gnn_W_comb", "L1_gnn_b_comb", "L2_gnn_W_nb", "L2_gnn_b_nb", "L2_gnn_W_line",
        "L2_gnn_b_line", "L3_gnn_W", "L3_gnn_a1", "L3_gnn_a2"]


def kernel(**inputs):
    import numpy as np
    import concourse.bacc as bacc
    from concourse.bass_utils import run_bass_kernel_spmd

    nc = bacc.Bacc("TRN2", target_bir_lowering=False, num_devices=1)
    arrays, args = {}, []
    for name in _INS:
        a = np.ascontiguousarray(inputs[name])
        arrays[f"in_{name}"] = a
        args.append(nc.dram_tensor(f"in_{name}", a.shape, mybir.dt.from_np(a.dtype), kind="ExternalInput").ap())
    args.append(nc.dram_tensor("out_x", (N, D), mybir.dt.float32, kind="ExternalOutput").ap())
    gnn_program(nc, *args)
    r = run_bass_kernel_spmd(nc, [arrays], core_ids=[0])
    return r.results[0]["out_x"]
```

```python
import concourse.bass as bass
from concourse import mybir
from contextlib import ExitStack

DT = mybir.dt
ALU = mybir.AluOpType
ACT = mybir.ActivationFunctionType
AX = mybir.AxisListType
RMAX = bass.bass_isa.ReduceOp.max

P = 128
N = 2708
D = 512
NT = (N + P - 1) // P
NP = NT * P
TAIL = N - (NT - 1) * P
KT = D // P
H, O = 8, 64
OC = O + 1
MC = 96
PB = D // MC
NB = (NT + PB - 1) // PB
KEEP = 64
EPS = 1e-5

H_SCALE = 2.0 ** 11
W_SCALE = 2.0 ** 8
Y_SCALE = 2.0 ** 8
UNSCALE = 1.0 / (H_SCALE * W_SCALE)
EDGE = 2.0


def pipeline(eng, stages, period=2, begin=None, until=None):
    high, low = max(l for l, _ in stages), min(l for l, _ in stages)
    first, last = period - low, NT - 2 - high
    turns = max(0, (last - first + 1) // period)

    def step(u, base):
        for lead, fn in stages:
            if isinstance(u, int):
                if 0 <= u + lead < NT:
                    fn(u + lead, (u + lead) % period)
            else:
                fn(u + lead, (base + lead) % period)

    for u in range(-high if begin is None else begin, first if until is None else until):
        step(u, u)
    if until is not None:
        return
    if turns > 0:
        with eng.Fori(first, first + (turns - 1) * period + 1, period) as u:
            for k in range(period):
                step(u + k, first + k)
    for u in range(first + turns * period, NT - low):
        step(u, u)


def inner(t, least):
    return not isinstance(t, int) or t >= least


def gnn_program(nc, x_in, adj, w_self0, w_neigh0, w_self1, b_self1, w_nb1, b_nb1, w_comb, b_comb,
                w_nb2, b_nb2, w_line2, b_line2, w3, a1, a2, out):
    ctx = ExitStack()
    with ctx:
        f32, f16, bf16, u8, i32 = DT.float32, DT.float16, DT.bfloat16, DT.uint8, DT.int32

        def sb(name, shape, dt):
            return ctx.enter_context(nc.sbuf_tensor(name, shape, dt))

        sems = {}

        def S(name):
            if name not in sems:
                sems[name] = ctx.enter_context(nc.semaphore(name))
            return sems[name]

        w_parts = nc.dram_tensor("w_parts", [5, P, 2 * KT * D], f16).ap()
        self_rows = nc.dram_tensor("self_rows", [NT, P, D], f32).ap()
        h0_row = nc.dram_tensor("h0_row", [NT, P], f32).ap()
        ratio_rows = nc.dram_tensor("ratio_rows", [H * NT, P], f32).ap()
        ratio_flat = ratio_rows.rearrange("a b -> (a b)")

        V = sb("neigh_code", [P, NT, NP], u8)
        X = sb("residual", [P, NT, D], f32)
        Yr = sb("products", [P, NT * H * OC + MC - OC], f32)
        Z = sb("arena", [P, 14080], f32)
        SMALL = sb("small", [P, 416], f32)

        def carve(region, byte, shape, dt):
            size = {f32: 4, i32: 4, f16: 2, bf16: 2, u8: 1}[dt]
            count = 1
            for n in shape:
                count *= n
            v = region[:, byte // 4: byte // 4 + (count * size + 3) // 4].bitcast(dt)
            if len(shape) == 1:
                return v
            names = "abcd"[:len(shape)]
            return v.rearrange(f"p ({' '.join(names)}) -> p {' '.join(names)}", **dict(zip(names[1:], shape[1:])))

        Vf = V[:, :, :].rearrange("p a b -> p (a b)").bitcast(f32)
        Xf = X[:, :, :].rearrange("p a b -> p (a b)")
        own0 = Yr[:, 0:NT * D].rearrange("p (t n) -> p t n", n=D)
        Y = Yr[:, 0:NT * D].bitcast(f16).rearrange("p (t s n) -> p t s n", s=2, n=D)
        Wh = Yr[:, 0:NT * H * OC].rearrange("p (h t o) -> p h t o", h=H, o=OC)

        Wt = carve(Z, 0, [2, 2, KT, D], f16)
        xn = carve(Z, 16384, [2, D], f32)
        h_hi = carve(Z, 20480, [2, D], f16)
        h_lo = carve(Z, 22528, [2, D], f16)
        hT = carve(Z, 24576, [2, 2 * KT, P], f16)
        stage = carve(Z, 28672, [2, D], f32)
        blk = carve(Z, 32768, [2, NT, P], bf16)
        x_stage = carve(Z, 32768, [4, D], f32)
        tmpa = carve(Z, 44032, [D], f32)
        tmpb = carve(Z, 46080, [D], f32)
        biasC = carve(Z, 48384, [D], f32)
        biasA = carve(Z, 51200, [D], f32)
        biasB = carve(Z, 53248, [D], f32)
        h0T = carve(Z, 50432, [P], f32)
        ident_f = carve(Z, 55296, [P], f32)
        ident_h = carve(Z, 55808, [P], f16)
        ident_b = carve(Z, 56064, [P], bf16)
        mask = carve(Z, 0, [2, NP], bf16)
        maskT = carve(Z, 11264, [2, NT, P], bf16)
        pick = carve(Z, 22528, [NT, P], bf16)
        h0_all = carve(Z, 28160, [NP], f32)
        junk_s = carve(Z, 39424, [2816], bf16)
        junk_v = carve(Z, 45056, [2816], bf16)
        adj_in = carve(Xf, 0, [4, N], i32)
        prob = [carve(Z, 11264 * k, [NP], f32) for k in range(3)]
        ratio = [carve(Z, 33792 + 11264 * k, [NP], f32) for k in range(2)]
        rT = carve(Z, 16384, [2, P], f32)
        ones_f = carve(Z, 17408, [P], f32)
        mean_lo = carve(Z, 33792 + 2 * 11264 - 4 * D, [D], f32)
        mean_hi = biasA
        f1 = carve(Z, 28672, [H, NT], f32)
        f2 = carve(Z, 29376, [H, NT], f32)
        fmax = carve(Z, 30080, [2, H], f32)
        gmax = carve(Z, 30144, [2, H], f32)
        zmax = carve(Z, 30208, [H], f32)
        guard = carve(Z, 30240, [H], f32)
        rbias = carve(Z, 30272, [H], f32)
        rexp = carve(Z, 30304, [H, NT], f32)
        barg = carve(Z, 31008, [H, NT], f32)
        dexp = carve(Z, 31712, [H, NT], f32)
        wh_sum = tmpb
        raw = carve(Xf, 0, [5, KT, D], f32)
        a12 = carve(Xf, 40960, [2, D], f32)
        wc = carve(Vf, 0, [2, KT, D], f32)
        wT = carve(Vf, 16384, [2, KT, D], f32)
        wP = carve(Vf, 32768, [KT, D], f32)
        parts = [carve(Vf, 40960 + 8192 * k, [2, KT, D], f16) for k in range(2)]
        bcols = carve(Vf, 57344, [KT, P], f32)
        rcols = carve(Vf, 59392, [KT, P], f32)
        bcol = carve(Vf, 61440, [2, KT], f32)
        rsum4 = carve(Vf, 61472, [KT], f32)
        fw32 = carve(Vf, 61488, [KT, 2 * H], f32)
        fw_tmp = rcols.rearrange("p a b -> p (a b)")
        s_col = carve(SMALL, 0, [NT], f32)
        rowsum = carve(SMALL, 88, [NT], f32)
        deg = carve(SMALL, 176, [NT], f32)
        rdeg = carve(SMALL, 264, [NT], f32)
        rcnt = carve(SMALL, 352, [NT], f32)
        has = carve(SMALL, 440, [NT], f32)
        iso = carve(SMALL, 528, [NT], f32)
        h0col = carve(SMALL, 616, [NT], f32)
        st6 = carve(SMALL, 704, [2, 6], f32)
        mv = carve(SMALL, 752, [2, 2], f32)
        veps = carve(SMALL, 768, [2, 1], f32)
        sd = carve(SMALL, 776, [2, 1], f32)
        rs = carve(SMALL, 784, [2, 1], f32)
        Fw = carve(SMALL, 792, [2, KT, 2 * H], f16)
        before = carve(SMALL, 1048, [NT + P], bf16)
        tri = carve(SMALL, 1348, [P], bf16)

        PS = ctx.enter_context(nc.psum_tensor("PS", [P, 8, D], f32))
        PSf = PS[:, :, :].rearrange("p a b -> p (a b)")
        spare = sb("spare", [P, 4], f32)
        small2 = sb("small2", [P, 352], f32)
        b_exp = carve(small2, 0, [H, NT], f32)
        d_neg = carve(small2, 704, [H, NT], f32)
        carry = carve(small2, 0, [2, P], bf16)

        block = ctx.enter_context(nc.Block())

        def everyone(eng, k):
            eng.drain().then_inc(S("phase"), 1)
            eng.wait_ge(S("phase"), 4 * k)

        SPLITS = [(0, 0, 0), (1, 1, 1), (2, 3, 2), (3, 4, 0), (4, 5, 0)]
        MATRIX = [m for _, m, _ in SPLITS]
        MATS = {1: [1, 3], 2: [4, 5], 3: [2]}

        def parts_of(m):
            return Wt[:, 0] if m == 0 else parts[m % 2]

        def rows(k):
            return P if k < NT - 1 else TAIL

        def parity_count(t, s):
            return 8 * (t - s) + 16

        def adj_count(t, s4):
            return 4 * (t - s4) + 16

        def unit(h2, hh, jt):
            return (2 * h2 + hh) * NT + jt

        def head_col(region, h2, hh, jt):
            return region[:, :, :].rearrange("p h t -> p (h t)")[:, bass.ds(unit(h2, hh, jt), 1)]

        def wh_tile(h2, hh, jt):
            return Yr[:, bass.ds(unit(h2, hh, jt) * OC, MC)]

        def heads(eng, work, before=None, extra={}):
            def head(h2, hh):
                n = 2 * h2 + hh
                if before:
                    before(h2, hh)
                for jt in range(3):
                    work(h2, hh, jt, (jt + hh) % 3)
                    if jt in extra and inner(n, 1):
                        extra[jt](n - 1)
                with eng.Fori(3, NT - 3, 3) as j:
                    for k in range(3):
                        work(h2, hh, j + k, (k + hh) % 3)
                if NT - 2 in extra and inner(n, 1):
                    extra[NT - 2](n - 1)
                work(h2, hh, NT - 1, (NT - 1 + hh) % 3)
            head(0, 0)
            head(0, 1)
            with eng.Fori(1, H // 2, 1) as h2:
                head(h2, 0)
                head(h2, 1)
            for jt in sorted(extra):
                extra[jt](H - 1)

        def project_dve(dve, l, part="all"):
            b0 = NT * l
            if l >= 2:
                dve.wait_ge(S("g_x"), NT * (l - 2) + 4 if part == "first tiles" else NT * (l - 1))

            def rows_of(t, s):
                return x_stage[:, s, :] if l == 0 else X[:, t, :]

            def add_sums(t, s4):
                dve.wait_ge(S(f"xr{s4}"), adj_count(t, s4))
                dve.scalar_tensor_tensor(tmpa[:, :], biasA[:, :], s_col[:, bass.ds(t, 1)], own0[:, t, :],
                                         ALU.mult, ALU.add).then_inc(S("p_t0"), 1)

            def add_relu(t, s4):
                dve.wait_ge(S("p_t0"), t + 1)
                dve.scalar_tensor_tensor(X[:, t, :], tmpa[:, :], 0.0, X[:, t, :], ALU.max, ALU.add)\
                    .then_inc(S("p_x1"), 1)

            def statistics(t, s4):
                if l == 0:
                    dve.wait_ge(S(f"x{s4}"), adj_count(t, s4))
                if l == 1:
                    dve.wait_ge(S("p_x1"), t + 1)
                dve.memset(spare[:, 0:1], 0.0)
                dve.bn_stats(st6[:, s4 % 2, :], rows_of(t, s4)).then_inc(S("p_st"), 1)

            def variance(t, s4):
                s = s4 % 2
                dve.wait_ge(S("p_st"), b0 + t + 1)
                dve.memset(spare[:, 1:2], 0.0)
                dve.bn_aggr(mv[:, s, :], st6[:, s, :]).then_inc(S("p_mv"), 1)

            def add_eps(t, s4):
                s = s4 % 2
                dve.wait_ge(S("p_mv"), b0 + t + 1)
                dve.tensor_scalar_add(veps[:, s, :], mv[:, s, 1:2], EPS).then_inc(S("p_var"), 1)

            def invert(t, s4):
                s = s4 % 2
                dve.wait_ge(S("p_sd"), b0 + t + 1)
                dve.reciprocal(rs[:, s, :], sd[:, s, :]).then_inc(S("p_rs"), 1)

            def normalise_rows(t, s4):
                s = s4 % 2
                dve.wait_ge(S("p_rs"), b0 + t + 1)
                dve.tensor_scalar(xn[:, s, :], rows_of(t, s4), mv[:, s, 0:1], rs[:, s, :], ALU.subtract, ALU.mult)\
                    .then_inc(S("p_xn"), 1)
                if l == 0:
                    dve.wait_ge(S("p_xn"), t + 1)
                    dve.tensor_scalar(h0col[:, bass.ds(t, 1)], xn[:, s, 0:1], 0.0, 1.0 / H_SCALE, ALU.max, ALU.mult)\
                        .then_inc(S("p_h0"), 1)

            def low_part(t, s4):
                s = s4 % 2
                dve.wait_ge(S("p_hi"), b0 + t + 1)
                if inner(t, 2):
                    dve.wait_ge(S("p_tr"), b0 + t - 1)
                dve.scalar_tensor_tensor(h_lo[:, s, :], xn[:, s, :], 0.0, h_hi[:, s, :], ALU.max, ALU.subtract)\
                    .then_inc(S("p_lo"), 1)

            def results(t, s4):
                s = s4 % 2
                if l in (1, 2) and isinstance(t, int) and t == NT - 1:
                    aggregate_dve(dve, l, "first tiles")
                if l < 3:
                    dve.wait_ge(S("p_mm"), b0 + t + 1)
                if l == 1:
                    if inner(t, 2):
                        dve.wait_ge(S(f"own_out{s}"), parity_count(t, s) - 16)
                    dve.scalar_tensor_tensor(stage[:, s, :], PS[:, 2 + s, :], UNSCALE, biasB[:, :],
                                             ALU.mult, ALU.add).then_inc(S("p_own"), 1)
                if l == 2:
                    if inner(t, 1):
                        dve.wait_ge(S("p_q3"), t)
                    dve.scalar_tensor_tensor(tmpa[:, :], PS[:, 2 + s, :], UNSCALE, biasA[:, :],
                                             ALU.mult, ALU.add).then_inc(S("p_q1"), 1)
                    dve.wait_ge(S("p_q1"), t + 1)
                    dve.scalar_tensor_tensor(tmpb[:, :], tmpa[:, :], 0.01, tmpa[:, :], ALU.mult, ALU.max)\
                        .then_inc(S("p_q2"), 1)
                    dve.wait_ge(S("p_q2"), t + 1)
                    dve.tensor_tensor(X[:, t, :], X[:, t, :], tmpb[:, :], ALU.add).then_inc(S("p_q3"), 1)
                if l == 3:
                    dve.wait_ge(S("p_f"), 2 * t + 2)
                    r = rows(t) if isinstance(t, int) else P
                    if inner(t, 1):
                        dve.wait_ge(S("wh_sum"), t)
                    total = wh_sum.rearrange("p (h o) -> p h o", o=O)
                    dve.tensor_tensor(total[0:r], Wh[0:r, :, t, 0:O], total[0:r], ALU.add).then_inc(S("wh_sum"), 1)
                    return
                dve.wait_ge(S("p_yhi"), b0 - NT + t + 1)
                dve.scalar_tensor_tensor(Y[:, t, 1, :], PS[:, 4 + s, :], Y_SCALE * UNSCALE, Y[:, t, 0, :],
                                         ALU.mult, ALU.subtract).then_inc(S("p_free"), 1)
            if l == 1:
                stages = [(4, add_sums), (3, invert), (4, add_relu), (3, normalise_rows), (4, statistics),
                          (2, low_part), (4, variance), (4, add_eps)]
            else:
                stages = [(4, statistics), (3, invert), (4, variance), (3, normalise_rows), (4, add_eps), (2, low_part)]
            if l > 0:
                stages.append((-2 if l == 3 else -1, results))
            if part == "first tiles":
                pipeline(dve, stages, until=0)
            else:
                pipeline(dve, stages, period=4 if l < 2 else 2, begin=0 if part == "rest" else None)

        def project_act(act, l):
            b0 = NT * l

            def deviation(t, s):
                act.wait_ge(S("p_var"), b0 + t + 1)
                act.activation(sd[:, s, :], veps[:, s, :], ACT.Sqrt, scale=1.0 / H_SCALE ** 2).then_inc(S("p_sd"), 1)

            def high_part(t, s):
                act.wait_ge(S("p_xn"), b0 + t + 1)
                if inner(t, 2):
                    act.wait_ge(S("p_tr"), b0 + t - 1)
                act.activation(h_hi[:, s, :], xn[:, s, :], ACT.Relu).then_inc(S("p_hi"), 1)

            def transposed(t, s):
                act.wait_ge(S("p_tr"), b0 + t + 1)
                if inner(t, 2):
                    act.wait_ge(S("p_mm"), b0 + t - 1)
                act.activation(hT[:, s].rearrange("p a b -> p (a b)"), PS[:, s, :].bitcast(f16), ACT.Copy)\
                    .then_inc(S("p_hT"), 1)

            def results(t, s):
                act.wait_ge(S("p_mm"), b0 + t + 1)
                if l == 0:
                    act.activation(own0[:, t, :], PS[:, 2 + s, :], ACT.Copy, scale=UNSCALE).then_inc(S("p_free"), 1)
                elif l < 3:
                    act.activation(Y[:, t, 0, :], PS[:, 4 + s, :], ACT.Copy, scale=Y_SCALE * UNSCALE)\
                        .then_inc(S("p_yhi"), 1)
                else:
                    act.activation(Wh[:, :, t, 0:O], PS[:, 2 + s, :].rearrange("p (h o) -> p h o", o=O), ACT.Copy,
                                   scale=UNSCALE).then_inc(S("p_f"), 1)
                    act.activation(f1[:, :, bass.ds(t, 1)], PS[:, 4 + s, 0:H].unsqueeze(2), ACT.Copy,
                                   scale=UNSCALE).then_inc(S("p_f"), 1)
                    act.activation(f2[:, :, bass.ds(t, 1)], PS[:, 4 + s, H:2 * H].unsqueeze(2), ACT.Copy,
                                   scale=UNSCALE).then_inc(S("p_free"), 1)
            pipeline(act, [(-1, results), (1, transposed), (4, deviation), (3, high_part)])

        def project_pe(pe, l):
            b0 = NT * l
            if l == 0:
                pe.wait_ge(S("w_lo"), 1)
            else:
                pe.wait_ge(S("wt"), 16 * sum(len(MATS[k]) for k in range(1, l + 1)))
            if l == 3:
                pe.wait_ge(S("fw_lo"), 1)

            def turn(t, s):
                pe.wait_ge(S("p_lo"), b0 + t + 1)
                if inner(t, 2):
                    pe.wait_ge(S("p_hT"), b0 + t - 1)
                for part, h in enumerate((h_hi, h_lo)):
                    for k in range(KT):
                        c = part * KT + k
                        ins = pe.transpose(PS[:, s, :].bitcast(f16)[:, c * P:(c + 1) * P],
                                           h[:, s, k * P:(k + 1) * P], ident_h[:, :])
                ins.then_inc(S("p_tr"), 1)

            def products(t, s):
                pe.wait_ge(S("p_hT"), b0 + t + 1)
                if inner(t, 2):
                    pe.wait_ge(S("p_free"), b0 + t - 1)
                outs = [(PS[:, 2 + s, :], lambda part, k: Wt[:, 0, part, k, :])]
                if l in (1, 2):
                    outs.append((PS[:, 4 + s, :], lambda part, k: Wt[:, 1, part, k, :]))
                if l == 3:
                    outs.append((PS[:, 4 + s, 0:2 * H], lambda part, k: Fw[:, part, k, :]))
                for hpart, wparts in ((0, (0, 1)), (1, (0,))):
                    for k in range(KT):
                        for dst, w in outs:
                            for wpart in wparts:
                                ins = pe.matmul(dst, hT[:, s, hpart * KT + k, :], w(wpart, k),
                                                start=hpart == 0 and k == 0 and wpart == 0,
                                                stop=hpart == 1 and k == KT - 1)
                ins.then_inc(S("p_mm"), 1)
            pipeline(pe, [(1, turn), (0, products)])

        def aggregate_dve(dve, l, part="rest"):
            b0 = NT * (l - 1)

            def neighbours(t, s):
                if inner(t, 2):
                    dve.wait_ge(S("g_mm"), b0 + t - 1)
                dve.tensor_scalar(blk[:, s], V[:, :, bass.ts(t, P)], 2.0, None,
                                  ALU.is_ge if l == 1 else ALU.is_equal).then_inc(S("g_blk"), 1)
                if l == 2:
                    dve.tensor_scalar(V[:, :, bass.ts(t, P)], V[:, :, bass.ts(t, P)], 2.0, None, ALU.is_ge)\
                        .then_inc(S("g_v"), 1)

            def update(t, s):
                if isinstance(t, int) and t == NT - 2:
                    project_dve(dve, l + 1, "first tiles")
                dve.wait_ge(S("g_mm"), b0 + t + 1)
                if inner(t, 1):
                    dve.wait_ge(S("g_x"), b0 + t)
                if l == 1:
                    dve.wait_ge(S(f"own_in{s}"), parity_count(t, s))
                    dve.scalar_tensor_tensor(tmpa[:, :], PS[:, 6 + s, :], rdeg[:, bass.ds(t, 1)], stage[:, s, :],
                                             ALU.mult, ALU.add).then_inc(S("g_t1"), 1)
                    dve.wait_ge(S("g_t1"), b0 + t + 1)
                    dve.scalar_tensor_tensor(X[:, t, :], tmpa[:, :], 0.0, X[:, t, :], ALU.max, ALU.add)\
                        .then_inc(S("g_x"), 1)
                else:
                    dve.scalar_tensor_tensor(tmpa[:, :], PS[:, 6 + s, :], rcnt[:, bass.ds(t, 1)], biasC[:, :],
                                             ALU.mult, ALU.add).then_inc(S("g_t1"), 1)
                    dve.wait_ge(S("g_t1"), b0 + t + 1)
                    dve.scalar_tensor_tensor(tmpb[:, :], tmpa[:, :], 0.01, tmpa[:, :], ALU.mult, ALU.max)\
                        .then_inc(S("g_t2"), 1)
                    dve.wait_ge(S("g_t2"), t + 1)
                    dve.scalar_tensor_tensor(X[:, t, :], tmpb[:, :], has[:, bass.ds(t, 1)], X[:, t, :],
                                             ALU.mult, ALU.add).then_inc(S("g_x"), 1)
            if part == "first tiles":
                pipeline(dve, [(1, neighbours), (-1, update)], until=0)
                return
            if l == 2:
                dve.wait_ge(S("p_q3"), NT)
            pipeline(dve, [(1, neighbours), (-1, update)], begin=0)

        def aggregate_pe(pe, l):
            b0 = NT * (l - 1)
            pe.wait_ge(S("p_free"), NT * (l + 1))

            def aggregate(t, s):
                pe.wait_ge(S("g_blk"), b0 + t + 1)
                if inner(t, 2):
                    pe.wait_ge(S("g_t1"), b0 + t - 1)
                for j in range(NT):
                    for part in range(2):
                        ins = pe.matmul(PS[:, 6 + s, :], blk[:, s, j, :], Y[:, j, part, :],
                                        start=j == 0 and part == 0, stop=j == NT - 1 and part == 1)
                ins.then_inc(S("g_mm"), 1)
            pipeline(pe, [(0, aggregate)])

        by_rows = "(t p) k -> p t k"

        @block.sync
        def _(sp):
            sp.dma_start(raw[:, 0], w_self0.rearrange(by_rows, p=P)).then_inc(S("raw0"), 16)

            def load_x(t, s4):
                if inner(t, 4):
                    sp.wait_ge(S("p_xn"), t - 3)
                if isinstance(t, int) and t == NT - 1:
                    sp.dma_start(x_stage[0:TAIL, s4, :], x_in[t * P:N, :]).then_inc(S(f"x{s4}"), 16)
                else:
                    sp.dma_start(x_stage[:, s4, :], x_in[bass.ts(t, P), :]).then_inc(S(f"x{s4}"), 16)
            pipeline(sp, [(0, load_x)], period=4)

            sp.dma_start(raw[:, 1], w_self1.rearrange(by_rows, p=P)).then_inc(S("raw1"), 16)
            sp.dma_start(wc[:, 0], w_comb[0:D, :].rearrange(by_rows, p=P)).then_inc(S("wc0"), 16)
            with nc.allow_non_contiguous_dma(reason="biases as columns"):
                sp.dma_start(bcol[:, 0, :], b_self1.rearrange("(t p) -> p t", p=P)).then_inc(S("bcol"), 16)
                sp.dma_start(bcol[:, 1, :], b_nb1.rearrange("(t p) -> p t", p=P)).then_inc(S("bcol"), 16)
            sp.dma_start(raw[:, 2], w_nb1.rearrange(by_rows, p=P)).then_inc(S("raw2"), 16)
            sp.dma_start(wc[:, 1], w_comb[D:2 * D, :].rearrange(by_rows, p=P)).then_inc(S("wc1"), 16)
            sp.dma_start(biasB[:, :], b_comb.partition_broadcast(P)).then_inc(S("biasB"), 16)
            sp.dma_start(raw[:, 3], w_line2.rearrange(by_rows, p=P)).then_inc(S("raw3"), 16)
            sp.dma_start(raw[:, 4], w_nb2.rearrange(by_rows, p=P)).then_inc(S("raw4"), 16)
            sp.dma_start(a12[:, 0, :], a1.rearrange("h o -> (h o)").partition_broadcast(P)).then_inc(S("a12"), 16)
            sp.dma_start(a12[:, 1, :], a2.rearrange("h o -> (h o)").partition_broadcast(P)).then_inc(S("a12"), 16)
            sp.wait_ge(S("w_tr"), KT)
            sp.dma_start(raw[:, 0], w_neigh0.rearrange(by_rows, p=P)).then_inc(S("raw0"), 16)
            sp.wait_ge(S("h0_sb"), 1)
            sp.dma_start(h0_row[:, :], h0T[0:NT, :]).then_inc(S("h0_dram"), 16)
            sp.wait_ge(S("h0_dram"), 16)
            sp.dma_start(h0_all[:, :], h0_row.rearrange("a b -> (a b)").partition_broadcast(P)).then_inc(S("h0_all"), 16)
            sp.wait_ge(S("w_tr"), 2 * KT)
            for k in range(KT):
                sp.dma_start(raw[:, 1, k, :].rearrange("p (h o) -> p h o", o=O),
                             w3[:, k * P:(k + 1) * P, :].rearrange("h p o -> p h o")).then_inc(S("raw1"), 16)

            for m in (1, 2, 3):
                sp.wait_ge(S("w_lo"), m + 1)
                sp.dma_start(w_parts[m - 1], parts_of(m).rearrange("p a b c -> p (a b c)"))\
                  .then_inc(S(f"w_out{m % 2}"), 16)
            sp.wait_ge(S("fw32"), 1)
            sp.wait_ge(S("rcols"), 1)
            sp.wait_ge(S("w_tr"), 5 * KT)

            def load_adj(t, s):
                if inner(t, 4):
                    sp.wait_ge(S("b_mask"), t - 3)
                    sp.wait_ge(S("b_rowsum"), t - 3)
                    sp.wait_ge(S("b_s"), t - 3)
                if isinstance(t, int) and t == NT - 1:
                    sp.dma_start(adj_in[0:TAIL, s, :], adj[t * P:N, :]).then_inc(S(f"adj{s}"), 16)
                else:
                    sp.dma_start(adj_in[:, s, :], adj[bass.ts(t, P), :]).then_inc(S(f"adj{s}"), 16)
            pipeline(sp, [(0, load_adj)], period=4)
            sp.wait_ge(S("w_out0"), 32)
            sp.wait_ge(S("w_out1"), 48)

            def load_weights(layer):
                for n, m in enumerate(MATS[layer]):
                    sp.dma_start(Wt[:, n].rearrange("p a b c -> p (a b c)"), w_parts[m - 1]).then_inc(S("wt"), 16)

            sp.wait_ge(S("b_mask"), NT)
            sp.wait_ge(S("x_clear"), 1)

            def load_x1(t, s):
                if inner(t, 4):
                    sp.wait_ge(S("p_x1"), t - 3)
                if isinstance(t, int) and t == NT - 1:
                    sp.dma_start(X[0:TAIL, t, :], x_in[t * P:N, :]).then_inc(S(f"xr{s}"), 16)
                else:
                    sp.dma_start(X[:, t, :], x_in[bass.ts(t, P), :]).then_inc(S(f"xr{s}"), 16)

            def store_own(t, s4):
                s = s4 % 2
                sp.wait_ge(S("p_own"), t + 1)
                sp.dma_start(self_rows[t], stage[:, s, :]).then_inc(S(f"own_out{s}"), 16)
            pipeline(sp, [(6, load_x1), (-1, store_own)], period=4, until=-2)
            sp.wait_ge(S("phase"), 8)
            load_weights(1)
            pipeline(sp, [(6, load_x1), (-1, store_own)], period=4, begin=-2)
            for s in range(2):
                sp.wait_ge(S(f"own_out{s}"), 16 * (NT // 2))

            def load_own(t, s):
                if inner(t, 2):
                    sp.wait_ge(S("g_t1"), t - 1)
                sp.dma_start(stage[:, s, :], self_rows[t]).then_inc(S(f"own_in{s}"), 16)
            sp.wait_ge(S("p_mm"), 2 * NT)
            load_weights(2)
            sp.dma_start(biasA[:, :], b_line2.partition_broadcast(P)).then_inc(S("bias2"), 16)
            sp.dma_start(biasC[:, :], b_nb2.partition_broadcast(P)).then_inc(S("bias2"), 16)
            pipeline(sp, [(0, load_own)])
            sp.wait_ge(S("p_mm"), 3 * NT)
            load_weights(3)

            sp.wait_ge(S("r_sb"), 2)
            sp.dma_start(ratio_rows[0:P, :], rT[:, 0, :]).then_inc(S("r_dram"), 16)
            sp.dma_start(ratio_rows[P:H * NT, :], rT[0:H * NT - P, 1, :]).then_inc(S("r_dram"), 16)
            sp.wait_ge(S("r_dram"), 32)

            def load_ratio(h, first, last):
                sp.dma_start(ratio[h % 2][:, first:last], ratio_flat[h * NP + first:h * NP + last].partition_broadcast(P))\
                  .then_inc(S(f"ratio{h % 2}"), 16)
            load_ratio(0, 0, NP)
            sp.wait_ge(S("x_iso"), 1)
            load_ratio(1, 0, NP - D)
            sp.wait_ge(S("x_iso"), NT)
            load_ratio(1, NP - D, NP)
            for h in range(2, H):
                sp.wait_ge(S("l_relu"), NT * (h - 1))
                load_ratio(h, 0, NP)
            for first, last in ((0, H - 2), (H - 2, H)):
                cols = slice(first * O, last * O)
                sp.wait_ge(S("l_x"), last)
                sp.dma_start(out[0:(NT - 1) * P, cols].rearrange("(t p) c -> p t c", p=P), X[:, 0:NT - 1, cols])\
                  .then_inc(S("out"), 16)
                sp.dma_start(out[(NT - 1) * P:N, cols], X[0:TAIL, NT - 1, cols]).then_inc(S("out"), 16)
            sp.wait_ge(S("out"), 64)

        @block.gpsimd
        def _(pool):
            for m in (ident_f, ident_h, ident_b):
                pool.memset(m[:, :], 0.0).then_inc(S("zeroed"), 1)
            pool.wait_ge(S("zeroed"), 3)
            for m in (ident_f, ident_h, ident_b):
                pool.affine_select(out=m[:, :], in_=m[:, :], compare_op=ALU.not_equal, fill=1.0,
                                   base=0, pattern=[[-1, P]], channel_multiplier=1).then_inc(S("ident"), 1)
            pool.wait_ge(S("p_mm"), NT)
            pool.memset(mask[:, :, N:NP], 0.0).then_inc(S("cst0"), 1)
            pool.memset(before[:, 0:NT], 0.0).then_inc(S("cst0"), 1)
            pool.memset(before[:, NT:NT + P], 1.0 / EDGE).then_inc(S("cst0"), 1)
            pool.memset(tri[:, 0:P], 1.0 / EDGE).then_inc(S("cst0"), 1)
            pool.memset(pick[:, :, :], 0.0).then_inc(S("cst0"), 1)
            pool.wait_ge(S("cst0"), 5)
            pool.affine_select(out=tri[:, 0:P], in_=tri[:, 0:P], compare_op=ALU.is_ge, fill=0.0,
                               base=0, pattern=[[1, P]], channel_multiplier=-1).then_inc(S("cst"), 1)
            pool.affine_select(out=pick[:, :, :], in_=pick[:, :, :], compare_op=ALU.not_equal, fill=1.0,
                               base=0, pattern=[[-1, NT], [0, P]], channel_multiplier=1).then_inc(S("cst"), 1)

            everyone(pool, 1)
            everyone(pool, 2)
            pool.wait_ge(S("fmax"), 2)
            pool.partition_all_reduce(gmax[:, :, :].rearrange("p a b -> p (a b)"),
                                      fmax[:, :, :].rearrange("p a b -> p (a b)"), P, RMAX).then_inc(S("gmax"), 1)
            everyone(pool, 3)

        @block.scalar
        def _(act):
            def weight_act(job, m, product):
                for k in range(KT):
                    act.wait_ge(S("w_tr"), job * KT + k + 1)
                    if k == 0 and job >= 2:
                        act.wait_ge(S("w_lo"), MATRIX[job - 2] + 1)
                    act.activation(wT[:, job % 2, k, :], PS[:, k % 2, :], ACT.Copy).then_inc(S("w_ev"), 1)
                src = wT[:, job % 2]
                if product:
                    for k in range(KT):
                        act.wait_ge(S("w_mm"), (product - 1) * KT + k + 1)
                        if k == 0 and product == 2:
                            act.wait_ge(S("w_lo"), MATRIX[1] + 1)
                        act.activation(wP[:, k, :], PS[:, 2 + k % 2, :], ACT.Copy).then_inc(S("w_pev"), 1)
                    src = wP
                    act.wait_ge(S("w_pev"), product * KT)
                else:
                    act.wait_ge(S("w_ev"), (job + 1) * KT)
                if m >= 3:
                    act.wait_ge(S(f"w_out{m % 2}"), 16 * ((m - 1) // 2))
                act.activation(parts_of(m)[:, 0], src, ACT.Copy, scale=W_SCALE).then_inc(S("w_hi"), 1)

            weight_act(*SPLITS[0])
            project_act(act, 0)
            act.wait_ge(S("h0_ps"), 1)
            act.activation(h0T[0:NT, :], PS[0:NT, 0, 0:P], ACT.Copy).then_inc(S("h0_sb"), 1)
            weight_act(*SPLITS[1])
            act.wait_ge(S("raw1"), 16 + 16 * KT)
            act.activation(parts_of(2)[:, 0], raw[:, 1], ACT.Copy, scale=W_SCALE).then_inc(S("w_hi"), 1)
            for job in SPLITS[2:]:
                weight_act(*job)
            for m in (4, 5):
                act.wait_ge(S("w_lo"), m + 1)
                act.dma_start(w_parts[m - 1], parts_of(m).rearrange("p a b c -> p (a b c)"))\
                   .then_inc(S(f"w_out{m % 2}"), 16)
            act.wait_ge(S("wsum_ps"), 1)
            act.activation(biasA[:, :], PS[:, 6, :], ACT.Copy).then_inc(S("wsum"), 1)
            act.wait_ge(S("fw32"), 1)
            act.activation(Fw[:, 0], fw32[:, :, :], ACT.Copy, scale=W_SCALE).then_inc(S("fw_hi"), 1)

            everyone(act, 1)

            def row_sum(t, s4):
                act.wait_ge(S(f"adj{s4}"), adj_count(t, s4))
                if inner(t, 1):
                    act.wait_ge(S("b_rowsum"), t)
                act.activation(junk_s[:, 0:N], adj_in[:, s4, :], ACT.Copy,
                               accum_out=rowsum[:, bass.ds(t, 1)]).then_inc(S("b_rowsum"), 1)

            def mask_out(t, s4):
                s = s4 % 2
                for g in range(3):
                    n = min(8, NT - 8 * g)
                    act.wait_ge(S("b_tr"), 3 * t + g + 1)
                    if g == 0 and inner(t, 2):
                        act.wait_ge(S("b_code"), 3 * t - 3)
                    act.activation(maskT[:, s, 8 * g:8 * g + n, :].rearrange("p a b -> p (a b)"),
                                   PS[:, g, :].bitcast(bf16)[:, 0:n * P], ACT.Copy, scale=EDGE).then_inc(S("b_maskT"), 1)
            pipeline(act, [(2, row_sum), (1, mask_out)], period=4)
            everyone(act, 2)

            project_act(act, 1)
            project_act(act, 2)
            project_act(act, 3)
            act.wait_ge(S("args"), 1)
            act.activation(rexp[:, :, :], rexp[:, :, :], ACT.Exp).then_inc(S("exps"), 1)
            act.activation(b_exp[:, :, :], barg[:, :, :], ACT.Exp).then_inc(S("exps"), 1)
            act.activation(dexp[:, :, :], dexp[:, :, :], ACT.Exp).then_inc(S("exps"), 1)
            for k in range(2):
                n = P if k == 0 else H * NT - P
                act.wait_ge(S("r_ps"), k + 1)
                act.activation(rT[0:n, k, :], PS[0:n, k, 0:P], ACT.Copy).then_inc(S("r_sb"), 1)
            act.wait_ge(S("mean_lo"), 1)
            act.activation(mean_lo[:, :], mean_lo[:, :], ACT.Exp).then_inc(S("mean_exp"), 1)
            everyone(act, 3)

            def relu(h2, hh, jt, slot):
                back = 2 if hh == 0 and isinstance(jt, int) and jt < 2 else 3
                act.wait_ge(S("prob_free"), unit(h2, hh, jt) + 4 - back)
                act.activation(prob[slot][:, :], ratio[hh][:, :], ACT.Relu,
                               bias=head_col(d_neg, h2, hh, jt), scale=head_col(b_exp, h2, hh, jt)).then_inc(S("l_relu"), 1)

            def elu_exp(n):
                act.wait_ge(S("l_min"), n + 1)
                slab = Wh[:, n, :, 0:O]
                act.activation(slab, slab, ACT.Exp).then_inc(S("l_exp"), 1)
            heads(act, relu, extra={NT - 2: elu_exp},
                  before=lambda h2, hh: act.wait_ge(S(f"ratio{hh}"), 16 * h2 + 16 * (1 + hh)))

        @block.vector
        def _(dve):
            links = [0]

            def link(ins):
                links[0] += 1
                ins.then_inc(S("link"), 1)
                dve.wait_ge(S("link"), links[0])

            def low(m, src):
                dve.wait_ge(S("w_hi"), m + 1)
                dve.scalar_tensor_tensor(parts_of(m)[:, 1].rearrange("p a b -> p (a b)"), src.rearrange("p a b -> p (a b)"),
                                         W_SCALE, parts_of(m)[:, 0].rearrange("p a b -> p (a b)"),
                                         ALU.mult, ALU.subtract).then_inc(S("w_lo"), 1)
            low(0, wT[:, 0])
            project_dve(dve, 0)
            dve.wait_ge(S("bcol"), 32)
            dve.tensor_copy(bcols[:, :, :], bcol[:, 0, :].unsqueeze(2).to_broadcast([P, KT, P])).then_inc(S("bcols"), 1)
            dve.wait_ge(S("w_bias"), 1)
            dve.tensor_copy(bcols[:, :, :], bcol[:, 1, :].unsqueeze(2).to_broadcast([P, KT, P])).then_inc(S("bcols"), 1)
            low(1, wP)
            low(2, raw[:, 1])
            dve.wait_ge(S("a12"), 32)
            dve.wait_ge(S("raw1"), 16 + 16 * KT)
            for a in range(2):
                for k in range(KT):
                    link(dve.tensor_tensor(fw_tmp[:, :], raw[:, 1, k, :], a12[:, a, :], ALU.mult))
                    link(dve.tensor_reduce(fw32[:, k, a * H:(a + 1) * H],
                                           fw_tmp[:, :].rearrange("p (h o) -> p h o", o=O), AX.X, ALU.add))
            dve.sem_inc(S("fw32"), 1)
            dve.wait_ge(S("raw0"), 32)
            link(dve.tensor_reduce(rsum4[:, :], raw[:, 0], AX.X, ALU.add))
            dve.tensor_copy(rcols[:, :, :], rsum4[:, :].unsqueeze(2).to_broadcast([P, KT, P])).then_inc(S("rcols"), 1)
            low(3, wP)
            dve.wait_ge(S("w_bias"), 2)
            dve.wait_ge(S("biasB"), 16)
            dve.scalar_tensor_tensor(biasB[:, :], PS[:, 7, :], 1.0, biasB[:, :], ALU.mult, ALU.add).then_inc(S("bias1"), 1)
            low(4, wT[:, 1])
            low(5, wT[:, 0])
            dve.wait_ge(S("fw_hi"), 1)
            dve.scalar_tensor_tensor(Fw[:, 1], fw32[:, :, :], W_SCALE, Fw[:, 0], ALU.mult, ALU.subtract)\
                .then_inc(S("fw_lo"), 1)
            everyone(dve, 1)

            def neighbour_sum(t, s4):
                if inner(t, 1):
                    dve.wait_ge(S("b_s"), t)
                else:
                    dve.wait_ge(S("h0_all"), 16)
                dve.scalar_tensor_tensor(junk_v[:, 0:N], adj_in[:, s4, :], 1.0, h0_all[:, 0:N], ALU.mult, ALU.mult,
                                         accum_out=s_col[:, bass.ds(t, 1)]).then_inc(S("b_s"), 1)

            def make_mask(t, s4):
                s = s4 % 2
                dve.wait_ge(S(f"adj{s4}"), adj_count(t, s4))
                if inner(t, 2):
                    dve.wait_ge(S("b_tr"), 3 * t - 3)
                dve.tensor_scalar(mask[:, s, 0:N], adj_in[:, s4, :], 0.0, None, ALU.is_gt).then_inc(S("b_mask"), 1)

            def counts_out(t, s4):
                dve.wait_ge(S("b_count"), t + 1)
                dve.tensor_copy(deg[:, bass.ds(t, 1)], PS[:, 7, P:P + 1])
                dve.tensor_scalar_min(carry[:, s4 % 2, :], PS[:, 7, 0:P], KEEP + 1.0).then_inc(S("b_carry"), 1)

            def code_out(t, s4):
                s = s4 % 2
                if not inner(t, 1):
                    dve.wait_ge(S("w_out0"), 32)
                    dve.wait_ge(S("w_out1"), 48)
                for g in range(3):
                    n = min(8, NT - 8 * g)
                    b = 3 + 2 * ((s + g) % 2)
                    dve.wait_ge(S("b_cum"), 3 * t + g + 1)
                    dve.scalar_tensor_tensor(
                        V[:, 8 * g:8 * g + n, bass.ts(t, P)],
                        PSf[:, b * D:b * D + n * P].rearrange("p (a b) -> p a b", b=P),
                        KEEP + 0.5, maskT[:, s, 8 * g:8 * g + n, :], ALU.is_gt, ALU.add)\
                        .then_inc(S("b_code"), 1)
            pipeline(dve, [(0, counts_out), (2, make_mask), (0, code_out), (1, neighbour_sum)], period=4)
            dve.wait_ge(S("b_rowsum"), NT)
            dve.wait_ge(S("b_s"), NT)
            dve.memset(X[:, NT - 1, :], 0.0).then_inc(S("x_clear"), 1)
            dve.wait_ge(S("b_carry"), NT)
            link(dve.scalar_tensor_tensor(s_col[:, :], rowsum[:, :], 0.0, s_col[:, :], ALU.is_gt, ALU.mult))
            link(dve.tensor_scalar(rdeg[:, :], deg[:, :], 1.0, Y_SCALE, ALU.max, ALU.mult))
            link(dve.reciprocal(rdeg[:, :], rdeg[:, :]))
            link(dve.tensor_scalar(rcnt[:, :], deg[:, :], float(KEEP), 1.0, ALU.min, ALU.max))
            link(dve.tensor_scalar(rcnt[:, :], rcnt[:, :], Y_SCALE, None, ALU.mult))
            link(dve.reciprocal(rcnt[:, :], rcnt[:, :]))
            link(dve.tensor_scalar(has[:, :], deg[:, :], 0.0, None, ALU.is_gt))
            link(dve.tensor_scalar(iso[:, :], has[:, :], -1.0, 1.0, ALU.mult, ALU.add))
            everyone(dve, 2)

            project_dve(dve, 1)
            aggregate_dve(dve, 1)
            dve.wait_ge(S("bias2"), 32)
            project_dve(dve, 2, "rest")
            aggregate_dve(dve, 2)
            link(dve.memset(Wh[:, :, :, O:OC], 1.0))
            link(dve.memset(Yr[:, NT * H * OC:NT * H * OC + MC - OC], 0.0))
            link(dve.memset(wh_sum[:, :], 0.0))
            project_dve(dve, 3, "rest")

            dve.wait_ge(S("p_free"), 4 * NT)
            dve.memset(ones_f[:, :], 1.0).then_inc(S("ones"), 1)
            for k, f in enumerate((f1, f2)):
                dve.tensor_reduce(fmax[:, k, :], f[:, :, :], AX.X, ALU.max).then_inc(S("fmax"), 1)
            dve.wait_ge(S("gmax"), 1)
            link(dve.tensor_tensor(zmax[:, :], gmax[:, 0, :], gmax[:, 1, :], ALU.add))
            link(dve.tensor_scalar(guard[:, :], zmax[:, :], 0.8, 0.0, ALU.mult, ALU.max))
            link(dve.tensor_scalar(guard[:, :], guard[:, :], -1.0, 60.0, ALU.mult, ALU.add))
            link(dve.scalar_tensor_tensor(rbias[:, :], gmax[:, 1, :], 0.8, guard[:, :], ALU.mult, ALU.add))
            link(dve.scalar_tensor_tensor(rexp[:, :, :], f1[:, :, :], 0.8,
                                          rbias[:, :].unsqueeze(2).to_broadcast([P, H, NT]), ALU.mult, ALU.add))
            link(dve.tensor_tensor(barg[:, :, :], f2[:, :, :],
                                   gmax[:, 1, :].unsqueeze(2).to_broadcast([P, H, NT]), ALU.subtract))
            link(dve.scalar_tensor_tensor(dexp[:, :, :], barg[:, :, :], 0.2,
                                          guard[:, :].unsqueeze(2).to_broadcast([P, H, NT]), ALU.mult, ALU.add))
            dve.sem_inc(S("args"), 1)
            dve.wait_ge(S("exps"), 3)
            link(dve.tensor_scalar(d_neg[:, :, :], dexp[:, :, :], -1.0, None, ALU.mult))
            dve.wait_ge(S("mean_ps"), 1)
            dve.wait_ge(S("r_ps"), 2)
            dve.tensor_scalar(mean_hi[:, :], PS[:, 2, :], 1.0 / N, 0.0, ALU.mult, ALU.max).then_inc(S("mean_hi"), 1)
            dve.tensor_scalar(mean_lo[:, :], PS[:, 2, :], 1.0 / N, 0.0, ALU.mult, ALU.min).then_inc(S("mean_lo"), 1)
            dve.wait_ge(S("mean_exp"), 1)
            dve.wait_ge(S("mean_hi"), 1)
            link(dve.scalar_tensor_tensor(mean_lo[:, :], mean_lo[:, :], -1.0, mean_hi[:, :], ALU.add, ALU.add))
            everyone(dve, 3)

            def masked(h2, hh, jt, slot):
                dve.wait_ge(S("l_relu"), unit(h2, hh, jt) + 1)
                dve.scalar_tensor_tensor(prob[slot][:, :], prob[slot][:, :], head_col(d_neg, h2, hh, jt),
                                         V[:, jt, :], ALU.subtract, ALU.mult).then_inc(S("l_prob"), 1)
                if isinstance(h2, int) and (h2, hh) == (0, 0):
                    dve.scalar_tensor_tensor(X[:, jt, :], mean_lo[:, :], iso[:, bass.ds(jt, 1)], X[:, jt, :],
                                             ALU.mult, ALU.add).then_inc(S("x_iso"), 1)

            def normalise(n):
                def sums(b):
                    g = min(PB, NT - PB * b)
                    return g, PS[:, b, 0:g * MC].rearrange("p (a c) -> p a c", c=MC), h0col[:, PB * b:PB * b + g]

                def divisor(b):
                    g, s, den = sums(b)
                    if b < NB - 1:
                        dve.wait_ge(S("bank_done"), (NB - 1) * n + b + 1)
                    else:
                        dve.wait_ge(S("prob_free"), NT * (n + 1) + 3)
                    if b == 0 and inner(n, 1):
                        dve.wait_ge(S("l_norm"), NB * n)
                    dve.tensor_scalar(den.unsqueeze(2), s[:, :, O:OC], 1e-37, None, ALU.max).then_inc(S("l_den"), 1)

                def inverse(b):
                    g, s, den = sums(b)
                    dve.wait_ge(S("l_den"), NB * n + b + 1)
                    dve.reciprocal(den, den).then_inc(S("l_rden"), 1)

                def quotient(b):
                    g, s, den = sums(b)
                    dve.wait_ge(S("l_rden"), NB * n + b + 1)
                    dve.tensor_tensor(Wh[:, n, PB * b:PB * b + g, 0:O], s[:, :, 0:O],
                                      den.unsqueeze(2).to_broadcast([P, g, O]), ALU.mult).then_inc(S("l_norm"), 1)

                divisor(0)
                inverse(0)
                for b in range(1, NB):
                    divisor(b)
                    quotient(b - 1)
                    inverse(b)
                quotient(NB - 1)

            def positive(n):
                dve.wait_ge(S("l_norm"), NB * (n + 1))
                if not inner(n, 1):
                    dve.wait_ge(S("x_iso"), NT)
                slab = Wh[:, n, :, 0:O]
                xh = X[:, :, bass.ts(n, O)]
                dve.scalar_tensor_tensor(xh, slab, 0.0, xh, ALU.max, ALU.add).then_inc(S("l_pos"), 1)
                dve.tensor_scalar(slab, slab, 0.0, None, ALU.min).then_inc(S("l_min"), 1)

            def finish(n):
                dve.wait_ge(S("l_exp"), n + 1)
                dve.wait_ge(S("l_pos"), n + 1)
                xh = X[:, :, bass.ts(n, O)]
                dve.scalar_tensor_tensor(xh, Wh[:, n, :, 0:O], -1.0, xh, ALU.add, ALU.add).then_inc(S("l_x"), 1)
            heads(dve, masked, extra={0: normalise, 2: positive, NT - 2: finish})

        @block.tensor
        def _(pe):
            pe.wait_ge(S("ident"), 3)

            def weight_pe(job, m, product):
                pe.wait_ge(S(f"raw{job}"), 16)
                for k in range(KT):
                    n = job * KT + k
                    if n >= 2:
                        pe.wait_ge(S("w_ev"), n - 1)
                    for o in range(KT):
                        ins = pe.transpose(PS[:, k % 2, o * P:(o + 1) * P], raw[:, job, o, k * P:(k + 1) * P],
                                           ident_f[:, :])
                    ins.then_inc(S("w_tr"), 1)
                if product:
                    pe.wait_ge(S("w_ev"), (job + 1) * KT)
                    pe.wait_ge(S(f"wc{product - 1}"), 16)
                    for k in range(KT):
                        q = (product - 1) * KT + k
                        if q >= 2:
                            pe.wait_ge(S("w_pev"), q - 1)
                        for c in range(KT):
                            ins = pe.matmul(PS[:, 2 + k % 2, :], wT[:, job % 2, c, k * P:(k + 1) * P], wc[:, product - 1, c, :],
                                            start=c == 0, stop=c == KT - 1)
                        ins.then_inc(S("w_mm"), 1)
                    pe.wait_ge(S("bcols"), product)
                    for c in range(KT):
                        ins = pe.matmul(PS[:, 7, :], bcols[:, c, :], wc[:, product - 1, c, :],
                                        start=product == 1 and c == 0, stop=product == 2 and c == KT - 1)
                    ins.then_inc(S("w_bias"), 1)

            weight_pe(*SPLITS[0])
            project_pe(pe, 0)
            pe.wait_ge(S("p_h0"), NT)
            pe.transpose(PS[0:NT, 0, 0:P], h0col[:, :], ident_f[:, :]).then_inc(S("h0_ps"), 1)
            pe.wait_ge(S("h0_sb"), 1)
            for job in SPLITS[1:]:
                weight_pe(*job)
            pe.wait_ge(S("rcols"), 1)
            for c in range(KT):
                ins = pe.transpose(PS[:, 6, c * P:(c + 1) * P], rcols[:, c, :], ident_f[:, :])
            ins.then_inc(S("wsum_ps"), 1)

            everyone(pe, 1)
            pe.wait_ge(S("cst"), 2)

            def mask_turn(t, s4):
                s = s4 % 2
                pe.wait_ge(S("b_mask"), t + 1)
                for g in range(3):
                    if inner(t, 1):
                        pe.wait_ge(S("b_maskT"), 3 * t - 2 + g)
                    for c in range(min(8, NT - 8 * g)):
                        j = 8 * g + c
                        ins = pe.transpose(PS[:, g, :].bitcast(bf16)[:, c * P:(c + 1) * P],
                                           mask[:, s, j * P:(j + 1) * P], ident_b[:, :])
                    ins.then_inc(S("b_tr"), 1)

            def tile_counts(t, s4):
                s = s4 % 2
                pe.wait_ge(S("b_maskT"), 3 * t + 3)
                if inner(t, 1):
                    pe.wait_ge(S("b_carry"), t)
                for j in range(NT):
                    pe.matmul(PS[:, 7, 0:P], before[:, NT - 1 - j:NT - 1 - j + P], maskT[:, s, j, :],
                              start=j == 0, stop=j == NT - 1)
                for j in range(NT):
                    ins = pe.matmul(PS[:, 7, P:P + 1], maskT[:, s, j, :], before[:, NT:NT + 1],
                                    start=j == 0, stop=j == NT - 1)
                ins.then_inc(S("b_count"), 1)

            def running(t, s4):
                s = s4 % 2
                pe.wait_ge(S("b_carry"), t + 1)
                for g in range(3):
                    n = min(8, NT - 8 * g)
                    b = 3 + 2 * ((s + g) % 2)
                    if not (isinstance(t, int) and 3 * t + g < 2):
                        pe.wait_ge(S("b_code"), 3 * t + g - 1)
                    for half in range((n + 3) // 4):
                        m = min(4, n - 4 * half)
                        j0 = 8 * g + 4 * half
                        pe.matmul(PS[:, b + half, 0:m * P], tri[:, 0:P], maskT[:, s, j0:j0 + m, :],
                                  start=True, stop=False, skip_group_check=True)
                        for c in range(m):
                            ins = pe.matmul(PS[:, b + half, c * P:(c + 1) * P], pick[:, j0 + c, :], carry[:, s, :],
                                            start=False, stop=c == m - 1, skip_group_check=True)
                    ins.then_inc(S("b_cum"), 1)
            pipeline(pe, [(1, mask_turn), (0, tile_counts), (0, running)], period=4)
            everyone(pe, 2)

            project_pe(pe, 1)
            aggregate_pe(pe, 1)
            project_pe(pe, 2)
            aggregate_pe(pe, 2)
            project_pe(pe, 3)
            pe.wait_ge(S("ones"), 1)
            pe.wait_ge(S("wh_sum"), NT)
            pe.matmul(PS[:, 2, :], ones_f[:, :], wh_sum[:, :], start=True, stop=True).then_inc(S("mean_ps"), 1)
            pe.wait_ge(S("exps"), 1)
            rflat = rexp[:, :, :].rearrange("p a b -> p (a b)")
            pe.transpose(PS[:, 0, 0:P], rflat[:, 0:P], ident_f[:, :]).then_inc(S("r_ps"), 1)
            pe.transpose(PS[0:H * NT - P, 1, 0:P], rflat[:, P:H * NT], ident_f[:, :]).then_inc(S("r_ps"), 1)
            pe.sem_inc(S("prob_free"), 3)
            everyone(pe, 3)

            def attend(h2, hh, jt, slot):
                pe.wait_ge(S("l_prob"), unit(h2, hh, jt) + 1)
                for i in range(NT):
                    b, c = i // PB, (i % PB) * MC
                    first = isinstance(jt, int) and jt == 0 and c == 0
                    if first and (not isinstance(h2, int) or 2 * h2 + hh >= 1):
                        pe.wait_ge(S("l_norm"), NB * (2 * h2 + hh - 1) + b + 1)
                    ins = pe.matmul(PS[:, b, c:c + MC], prob[slot][:, i * P:(i + 1) * P], wh_tile(h2, hh, jt),
                                    start=first, stop=False, skip_group_check=True)
                    if isinstance(jt, int) and jt == NT - 1 and i % PB == PB - 1:
                        ins.then_inc(S("bank_done"), 1)
                ins.then_inc(S("prob_free"), 1)

            heads(pe, attend)


_INS = ["x", "adj", "L0_gnn_w_self", "L0_gnn_w_neigh", "L1_gnn_W_self", "L1_gnn_b_self", "L1_gnn_W_nb",
        "L1_gnn_b_nb", "L1_gnn_W_comb", "L1_gnn_b_comb", "L2_gnn_W_nb", "L2_gnn_b_nb", "L2_gnn_W_line",
        "L2_gnn_b_line", "L3_gnn_W", "L3_gnn_a1", "L3_gnn_a2"]


def kernel(**inputs):
    import numpy as np
    import concourse.bacc as bacc
    from concourse.bass_utils import run_bass_kernel_spmd

    nc = bacc.Bacc("TRN2", target_bir_lowering=False, num_devices=1)
    arrays, args = {}, []
    for name in _INS:
        a = np.ascontiguousarray(inputs[name])
        arrays[f"in_{name}"] = a
        args.append(nc.dram_tensor(f"in_{name}", a.shape, mybir.dt.from_np(a.dtype), kind="ExternalInput").ap())
    args.append(nc.dram_tensor("out_x", (N, D), mybir.dt.float32, kind="ExternalOutput").ap())
    gnn_program(nc, *args)
    r = run_bass_kernel_spmd(nc, [arrays], core_ids=[0])
    return r.results[0]["out_x"]
```
